# Optimizing a Trainium2 kernel written in Bass

```python
import numpy as np
import jax
import jax.numpy as jnp

def _softmax(x, axis=-1):
    return jax.nn.softmax(x, axis=axis)

def _gelu(x):
    return jax.nn.gelu(x, approximate=True)

def _silu(x):
    return jax.nn.silu(x)

def _sigmoid(x):
    return jax.nn.sigmoid(x)

def _layernorm(x, axis=-1, eps=1e-05):
    m = jnp.mean(x, axis=axis, keepdims=True)
    v = jnp.var(x, axis=axis, keepdims=True)
    return (x - m) / jnp.sqrt(v + eps)

def _scatter_add(tgt, idx, src, axis=0):
    return tgt.at[idx].add(src)

def _segment_sum(src, seg, n):
    return jax.ops.segment_sum(src, seg, n)
kernel_name = 'mk_xattn_ffn_d1_seqx_r8_26cd4e'

def setup_inputs(seed: int=0):
    np.random.seed(seed)
    _w = jnp.asarray

    def _rec_inputs():
        import jax
        import jax.numpy as jnp
        _rk = jax.random.key(seed)
        x = -0.0002928 + 1 * jax.random.normal(jax.random.fold_in(_rk, 1), (8, 128, 128), jnp.float32)
        _lenS = 128 - jax.random.randint(jax.random.fold_in(_rk, 7), (8,), 0, max(1, 128 // 4) + 1, jnp.int32)
        _lenS2 = 77 - jax.random.randint(jax.random.fold_in(_rk, 8), (8,), 0, max(1, 77 // 4) + 1, jnp.int32)
        _ctx_1024P = jax.random.normal(jax.random.fold_in(_rk, 11), (8, 16, 128), jnp.float32)
        _ctx_1024c = jax.random.dirichlet(jax.random.fold_in(_rk, 511), 0.3 * jnp.ones((16,), jnp.float32), (8, 77))
        _ctx_1024t = jnp.einsum('bsk,bkd->bsd', _ctx_1024c, _ctx_1024P)
        _ctx_1024t = _ctx_1024t * jax.lax.rsqrt(jnp.mean(jnp.square(_ctx_1024t)) + 1e-12) * 0.953939
        ctx_1024 = -1.39393e-06 + 0.999914 * (_ctx_1024t + 0.3 * jax.random.normal(jax.random.fold_in(_rk, 611), (8, 77, 128), jnp.float32))
        return (x, ctx_1024)
    x, ctx_1024 = _rec_inputs()

    def _L0_xattn_setup():
        import jax, jax.numpy as jnp
        import numpy as np
        NUM_HEADS = 16
        key = jax.random.key(seed)
        ks = jax.random.split(key, 6)
        b, s, d = (2, 256, 128)
        scale = 1.0 / np.sqrt(d)
        return {'x': jax.random.normal(ks[0], (b, s, d), dtype=jnp.float32), 'y': jax.random.normal(ks[1], (b, s, d), dtype=jnp.float32), 'wq': jax.random.normal(ks[2], (d, d), dtype=jnp.float32) * scale, 'wk': jax.random.normal(ks[3], (d, d), dtype=jnp.float32) * scale, 'wv': jax.random.normal(ks[4], (d, d), dtype=jnp.float32) * scale, 'wproj': jax.random.normal(ks[5], (d, d), dtype=jnp.float32) * scale}
    _L0_xattn_all = _L0_xattn_setup()
    _L0_xattn_in = {k: v for k, v in _L0_xattn_all.items() if k in ('wq', 'wk', 'wv', 'wproj')}
    del _L0_xattn_all

    def _L0_ffn_setup():
        import jax, jax.numpy as jnp
        import numpy as np
        N_EXPERTS = 32
        TOP_K = 8
        N_GROUP = 4
        TOPK_GROUP = 2
        ROUTED_SCALING = 2.5

        def _gate(x, gate_w, gate_bias):
            T, E = (x.shape[0], gate_w.shape[0])
            logits = jnp.einsum('th,eh->te', x, gate_w)
            scores = jax.nn.sigmoid(logits)
            scores_choice = scores + gate_bias[None, :]
            grp = scores_choice.reshape(T, N_GROUP, E // N_GROUP)
            top2, _ = jax.lax.top_k(grp, 2)
            group_scores = top2.sum(-1)
            _, grp_idx = jax.lax.top_k(group_scores, TOPK_GROUP)
            group_mask = jax.nn.one_hot(grp_idx, N_GROUP, dtype=scores.dtype).sum(1)
            expert_mask = jnp.repeat(group_mask, E // N_GROUP, axis=1)
            masked = jnp.where(expert_mask > 0, scores_choice, 0.0)
            _, topk_idx = jax.lax.top_k(masked, TOP_K)
            topk_w = jnp.take_along_axis(scores, topk_idx, axis=1)
            topk_w = topk_w / (topk_w.sum(-1, keepdims=True) + 1e-20)
            topk_w = topk_w * ROUTED_SCALING
            return (topk_idx, topk_w)

        def _mlp(x, wg, wu, wd):
            return jnp.einsum('...i,hi->...h', jax.nn.silu(jnp.einsum('...h,ih->...i', x, wg)) * jnp.einsum('...h,ih->...i', x, wu), wd)
        key = jax.random.key(seed)
        ks = jax.random.split(key, 9)
        B, S, H, I = (2, 64, 128, 64)
        w = 0.02
        return {'hidden_states': jax.random.normal(ks[0], (B, S, H), jnp.float32), 'gate_w': jax.random.normal(ks[1], (N_EXPERTS, H), jnp.float32) * w, 'gate_bias': jax.random.normal(ks[2], (N_EXPERTS,), jnp.float32) * w, 'expert_gate': jax.random.normal(ks[3], (N_EXPERTS, I, H), jnp.float32) * w, 'expert_up': jax.random.normal(ks[4], (N_EXPERTS, I, H), jnp.float32) * w, 'expert_down': jax.random.normal(ks[5], (N_EXPERTS, H, I), jnp.float32) * w, 'shared_gate': jax.random.normal(ks[6], (2 * I, H), jnp.float32) * w, 'shared_up': jax.random.normal(ks[7], (2 * I, H), jnp.float32) * w, 'shared_down': jax.random.normal(ks[8], (H, 2 * I), jnp.float32) * w}
    _L0_ffn_all = _L0_ffn_setup()
    _L0_ffn_in = {k: v for k, v in _L0_ffn_all.items() if k in ('gate_w', 'gate_bias', 'expert_gate', 'expert_up', 'expert_down', 'shared_gate', 'shared_up', 'shared_down')}
    del _L0_ffn_all
    return {'x': x, 'ctx_1024': ctx_1024, 'L0_xattn_wq': _L0_xattn_in['wq'], 'L0_xattn_wk': _L0_xattn_in['wk'], 'L0_xattn_wv': _L0_xattn_in['wv'], 'L0_xattn_wproj': _L0_xattn_in['wproj'], 'L0_ffn_gate_w': _L0_ffn_in['gate_w'], 'L0_ffn_gate_bias': _L0_ffn_in['gate_bias'], 'L0_ffn_expert_gate': _L0_ffn_in['expert_gate'], 'L0_ffn_expert_up': _L0_ffn_in['expert_up'], 'L0_ffn_expert_down': _L0_ffn_in['expert_down'], 'L0_ffn_shared_gate': _L0_ffn_in['shared_gate'], 'L0_ffn_shared_up': _L0_ffn_in['shared_up'], 'L0_ffn_shared_down': _L0_ffn_in['shared_down']}

def reference(x, ctx_1024, L0_xattn_wq, L0_xattn_wk, L0_xattn_wv, L0_xattn_wproj, L0_ffn_gate_w, L0_ffn_gate_bias, L0_ffn_expert_gate, L0_ffn_expert_up, L0_ffn_expert_down, L0_ffn_shared_gate, L0_ffn_shared_up, L0_ffn_shared_down):
    import jax
    import jax.numpy as jnp

    def _L0_xattn_ref(x, y, wq, wk, wv, wproj):
        import jax, jax.numpy as jnp
        import numpy as np
        NUM_HEADS = 16
        b, s, d = x.shape
        s_kv = y.shape[1]
        h = NUM_HEADS
        hd = d // h
        q = x @ wq.T
        k = y @ wk.T
        v = y @ wv.T
        q = q.reshape(b, h, s, hd)
        k = k.reshape(b, h, s_kv, hd)
        v = v.reshape(b, h, s_kv, hd)
        scores = jnp.einsum('bhqd,bhkd->bhqk', q, k) / jnp.sqrt(jnp.float32(hd))
        mask = jnp.triu(jnp.ones((s, s_kv), dtype=bool), k=1)
        scores = jnp.where(mask, -jnp.inf, scores)
        attn = jax.nn.softmax(scores, axis=-1)
        ctx = jnp.einsum('bhqk,bhkd->bhqd', attn, v)
        ctx = ctx.reshape(b, s, h * hd)
        return ctx @ wproj.T

    def _L0_ffn_ref(hidden_states, gate_w, gate_bias, expert_gate, expert_up, expert_down, shared_gate, shared_up, shared_down):
        import jax, jax.numpy as jnp
        import numpy as np
        N_EXPERTS = 32
        TOP_K = 8
        N_GROUP = 4
        TOPK_GROUP = 2
        ROUTED_SCALING = 2.5

        def _gate(x, gate_w, gate_bias):
            T, E = (x.shape[0], gate_w.shape[0])
            logits = jnp.einsum('th,eh->te', x, gate_w)
            scores = jax.nn.sigmoid(logits)
            scores_choice = scores + gate_bias[None, :]
            grp = scores_choice.reshape(T, N_GROUP, E // N_GROUP)
            top2, _ = jax.lax.top_k(grp, 2)
            group_scores = top2.sum(-1)
            _, grp_idx = jax.lax.top_k(group_scores, TOPK_GROUP)
            group_mask = jax.nn.one_hot(grp_idx, N_GROUP, dtype=scores.dtype).sum(1)
            expert_mask = jnp.repeat(group_mask, E // N_GROUP, axis=1)
            masked = jnp.where(expert_mask > 0, scores_choice, 0.0)
            _, topk_idx = jax.lax.top_k(masked, TOP_K)
            topk_w = jnp.take_along_axis(scores, topk_idx, axis=1)
            topk_w = topk_w / (topk_w.sum(-1, keepdims=True) + 1e-20)
            topk_w = topk_w * ROUTED_SCALING
            return (topk_idx, topk_w)

        def _mlp(x, wg, wu, wd):
            return jnp.einsum('...i,hi->...h', jax.nn.silu(jnp.einsum('...h,ih->...i', x, wg)) * jnp.einsum('...h,ih->...i', x, wu), wd)
        orig_shape = hidden_states.shape
        H = orig_shape[-1]
        residuals = hidden_states
        x = hidden_states.reshape(-1, H)
        topk_idx, topk_w = _gate(x, gate_w, gate_bias)
        g = jnp.einsum('th,eih->eti', x, expert_gate)
        u = jnp.einsum('th,eih->eti', x, expert_up)
        outs = jnp.einsum('eti,ehi->eth', jax.nn.silu(g) * u, expert_down)
        outs_t = jnp.transpose(outs, (1, 0, 2))
        gathered = jnp.take_along_axis(outs_t, topk_idx[:, :, None], axis=1)
        final = (gathered * topk_w[:, :, None]).sum(1)
        shared = _mlp(residuals, shared_gate, shared_up, shared_down)
        return final.reshape(orig_shape) + shared
    x = x + _L0_xattn_ref(_layernorm(x, axis=-1), ctx_1024, L0_xattn_wq, L0_xattn_wk, L0_xattn_wv, L0_xattn_wproj)
    x = x + _L0_ffn_ref(_layernorm(x, axis=-1), L0_ffn_gate_w, L0_ffn_gate_bias, L0_ffn_expert_gate, L0_ffn_expert_up, L0_ffn_expert_down, L0_ffn_shared_gate, L0_ffn_shared_up, L0_ffn_shared_down)
    return x

_drawn_inputs = setup_inputs


def setup_inputs(seed=0):
    import zlib

    import numpy as np

    out = dict(_drawn_inputs(seed))
    spreads = {}
    factors = {'L0_ffn_gate_w': 8.0,
     'L0_ffn_gate_bias': 8.0,
     'L0_ffn_expert_gate': 8.0,
     'L0_ffn_expert_up': 8.0,
     'L0_ffn_expert_down': 8.0,
     'L0_ffn_shared_gate': 8.0,
     'L0_ffn_shared_up': 8.0,
     'L0_ffn_shared_down': 8.0}
    for name, (base, spread) in spreads.items():
        noise = np.random.default_rng([zlib.crc32(name.encode()), seed]).standard_normal(out[name].shape)
        drawn = base * np.exp(spread * noise) if base else spread * noise
        out[name] = jnp.asarray(drawn.astype(out[name].dtype))
    for name, factor in factors.items():
        out[name] = (out[name] * factor).astype(out[name].dtype)
    return out
```

```python
from contextlib import ExitStack

import concourse.bass as bass
from concourse import mybir

ALU = mybir.AluOpType
ACT = mybir.ActivationFunctionType
AX = mybir.AxisListType
F32 = mybir.dt.float32
I32 = mybir.dt.int32
BF16 = mybir.dt.bfloat16
F16 = mybir.dt.float16

P = 128
D = 128
B, S, SKV = 8, 128, 77
NH, HD = 16, 8
HALVES = 2
BH = B // HALVES * NH
TOK = B // HALVES * S
KV = B // HALVES * SKV
RR = S // NH
RL = TOK // P
C = D // HD
NKEY = SKV * C
GROUPS = 2
GH = BH // GROUPS
GP = 64
CH = 4
CHUNKS = GH // CH
NE = 32
NG = 4
TOPK = 8
PAIRS = NE // 2
UNITS = PAIRS + 1
ROUTED_SCALING = 2.5
EPS = 1e-5
SCALE = float(HD) ** -0.5
LN4096 = 8.317766166719343
Q_PART = [0, 0, 1, 0, 2, 1]
K_PART = [0, 1, 0, 2, 0, 1]
SLOTS = len(Q_PART)
ROWS = SLOTS * HD
VC = 3 * HD + 1


def block_kernel(nc, x, ctxT, wattn, gwT, gbias, eg, eu, ed, cf32, cbf16, cf16, csel, out):
    with ExitStack() as ctx:
        def sb(name, shape, dt=F32):
            return ctx.enter_context(nc.sbuf_tensor(name, shape, dt))

        def sem(name):
            return ctx.enter_context(nc.semaphore(name))

        x_sb = sb("x_sb", [P, HALVES, RL, D])
        ctx_sb = sb("ctx_sb", [P, HALVES, KV])
        wat = sb("wat", [P, 4, D])
        gw = sb("gw", [P, NE])
        gb = sb("gb", [P, NE])
        egs = sb("egs", [P, UNITS, P])
        eus = sb("eus", [P, UNITS, P])
        eds = sb("eds", [P, UNITS, P])
        cf = sb("cf", [P, P + NG * NG])
        cb = sb("cb", [P, P + CH * SKV], BF16)
        ch = sb("ch", [P, P], F16)
        sel = sb("sel", [3 * NE, PAIRS, P], BF16)
        identf = cf[:, 0:P]
        lower = cf[:, P:P + NG * NG]
        identb = cb[:, 0:P]
        maskneg = cb[:, P:P + CH * SKV]

        stats = sb("stats", [P, RL, 6])
        mv = sb("mv", [P, RL, 2])
        lnv = sb("lnv", [P, RL])
        lni = sb("lni", [P, RL], I32)
        lny = sb("lny", [P, RL])
        lnt = sb("lnt", [P, RL])
        xn = sb("xn", [P, RL, D])
        xnT = sb("xnT", [P, HALVES, TOK])
        xn2T = sb("xn2T", [P, HALVES, TOK])

        QT = sb("QT", [P, HALVES, 3, TOK], BF16)
        KT = sb("KT", [P, HALVES, 3, KV], BF16)
        VT = sb("VT", [P, HALVES, KV])
        res = sb("res", [P, TOK])
        QS = sb("QS", [GP + ROWS, HALVES, C * RR, GH], BF16)
        KS = sb("KS", [GP + ROWS, HALVES, C, 2 * SKV], BF16)
        KR = sb("KR", [GP + ROWS, HALVES, 2, NKEY], BF16)
        VS = sb("VS", [4 * HD, HALVES, C, SKV])
        VR = sb("VR", [4 * HD, HALVES, NKEY])
        VV = sb("VV", [SKV, HALVES, BH, VC], BF16)
        vres = sb("vres", [SKV, 4 * P])
        mx = sb("mx", [P, 2, GROUPS * CH])
        Sm = sb("Sm", [P, 2, GROUPS, CH, SKV])
        Ph = sb("Ph", [P, 2, GROUPS, CH, SKV], F16)
        P32 = sb("P32", [P, 2, GROUPS, CH, SKV])
        Pl = sb("Pl", [P, 2, GROUPS, CH, SKV], F16)
        PT = sb("PT", [SKV, 2, 2, GROUPS * CH * P], F16)
        osum = sb("osum", [P, GROUPS, 8, HD])
        oden = sb("oden", [P, GROUPS, 8])
        On = sb("On", [P, HALVES, HD, BH])
        CT = sb("CT", [P, HALVES, RR, BH])
        x1 = sb("x1", [P, HALVES, RL, D])
        bias12 = sb("bias12", [P, 1])

        ge = sb("ge", [P, RL, NE])
        gs = sb("gs", [P, RL, NE])
        gsc = sb("gsc", [P, RL, NE])
        th = sb("th", [P, 6, RL * NG * 4])
        grp = sb("grp", [P, RL, NG])
        cmp = sb("cmp", [P, 3, RL, NG, NG])
        gcnt = sb("gcnt", [P, RL, NG])
        msk = sb("msk", [P, RL, NE])
        top8 = sb("top8", [P, RL, 8])
        repl = sb("repl", [P, RL, NE])
        wgt = sb("wgt", [P, RL, NE])
        wsum = sb("wsum", [P, RL])
        w3 = sb("w3", [P, RL, 3, NE], BF16)
        wres = sb("wres", [P, RL, NE])
        W3T = sb("W3T", [3 * NE, HALVES, TOK], BF16)

        sg = sb("sg", [P, 2, TOK])
        h1 = sb("h1", [P, 2, TOK])
        hw = sb("hw", [P, 2, TOK])
        yT = sb("yT", [P, TOK])
        y = sb("y", [P, HALVES, RL, D])

        ps = ctx.enter_context(nc.psum_tensor("ps", [P, 8, 512], F32))

        s_cf = sem("s_cf")
        s_x = [sem(f"s_x{i}") for i in range(HALVES)]
        s_ctx = sem("s_ctx")
        s_gw = sem("s_gw")
        s_eg = sem("s_eg")
        s_cb = sem("s_cb")
        gap_zero = sem("gap_zero")
        consts_set = sem("consts_set")
        dve = sem("dve")
        xn_ready = sem("xn_ready")
        xnT_psum = sem("xnT_psum")
        xnT_ready = sem("xnT_ready")
        k_psum = sem("k_psum")
        v_psum = sem("v_psum")
        q_psum = sem("q_psum")
        k_split = sem("k_split")
        v_copied = sem("v_copied")
        q_split = sem("q_split")
        k_spread = [sem(f"k_spread{i}") for i in range(HALVES)]
        v_spread = [sem(f"v_spread{i}") for i in range(HALVES)]
        q_spread = [sem(f"q_spread{i}") for i in range(HALVES)]
        k_ordered = sem("k_ordered")
        v_ordered = sem("v_ordered")
        vT_psum = sem("vT_psum")
        v_split = sem("v_split")
        scores_ready = sem("scores_ready")
        scores_used = sem("scores_used")
        exps_ready = sem("exps_ready")
        low_ready = sem("low_ready")
        pT_psum = sem("pT_psum")
        pT_high = sem("pT_high")
        pT_low = sem("pT_low")
        pv_ready = sem("pv_ready")
        o_ready = sem("o_ready")
        c_spread = [sem(f"c_spread{i}") for i in range(HALVES)]
        proj_psum = sem("proj_psum")
        x1_ready = sem("x1_ready")
        xn2_ready = sem("xn2_ready")
        xn2T_psum = sem("xn2T_psum")
        xn2T_ready = sem("xn2T_ready")
        logits_psum = sem("logits_psum")
        gexp_ready = sem("gexp_ready")
        w3_ready = sem("w3_ready")
        w3T_psum = sem("w3T_psum")
        w3T_ready = sem("w3T_ready")
        g_psum = sem("g_psum")
        u_psum = sem("u_psum")
        wb_psum = sem("wb_psum")
        silu_ready = sem("silu_ready")
        h_ready = sem("h_ready")
        down_done = sem("down_done")
        yT_ready = sem("yT_ready")
        y_psum = sem("y_psum")
        y_ready = sem("y_ready")
        s_out = sem("s_out")

        def token_view(t, hf, rh):
            v = t.rearrange("(f n) s d -> f (n s) d", f=HALVES)[hf]
            return v.rearrange("(a h l) d -> h a l d", h=2, l=RL)[rh]

        def spread_sizes():
            return 16 * SLOTS * GROUPS

        block = ctx.enter_context(nc.Block())

        @block.sync
        def _(sp):
            for hf in range(HALVES):
                for rh in range(2):
                    sp.dma_start(x_sb[64 * rh:64 * rh + 64, hf], token_view(x, hf, rh)).then_inc(s_x[hf], 16)
                if hf == 0:
                    sp.dma_start(cf[:, :], cf32).then_inc(s_cf, 16)
                    sp.dma_start(ctx_sb[:, :, :], ctxT).then_inc(s_ctx, 16)
                    sp.dma_start(wat[:, :, :], wattn).then_inc(s_ctx, 16)
            sp.dma_start(cb[:, :], cbf16).then_inc(s_cb, 16)
            sp.dma_start(ch[:, :], cf16).then_inc(s_cb, 16)
            sp.wait_ge(gap_zero, 1)
            for hf in range(HALVES):
                sp.wait_ge(k_split, hf + 1)
                for g in range(GROUPS):
                    for s in range(SLOTS):
                        sp.dma_start(KS[GP * g + HD * s:GP * g + HD * (s + 1), hf],
                                     KT[:, hf, K_PART[s], 2 * SKV * g:2 * SKV * (g + 1)]).then_inc(k_spread[hf], 16)
                sp.wait_ge(v_copied, hf + 1)
                for b in range(4):
                    sp.dma_start(VS[HD * b:HD * (b + 1), hf],
                                 VT[:, hf, SKV * b:SKV * (b + 1)]).then_inc(v_spread[hf], 16)
                sp.wait_ge(q_split, hf + 1)
                for g in range(GROUPS):
                    for s in range(SLOTS):
                        sp.dma_start(QS[GP * g + HD * s:GP * g + HD * (s + 1), hf],
                                     QT[:, hf, Q_PART[s], GH * RR * g:GH * RR * (g + 1)]).then_inc(q_spread[hf], 16)
            sp.dma_start(gw[:, :], gwT).then_inc(s_gw, 16)
            sp.dma_start(gb[:, :], gbias.partition_broadcast(P)).then_inc(s_gw, 16)
            sp.dma_start(sel[:, :, :], csel).then_inc(s_gw, 16)
            for dst, src in ((egs, eg), (eus, eu), (eds, ed)):
                sp.dma_start(dst[:, :, :], src).then_inc(s_eg, 16)
            for hf in range(HALVES):
                sp.wait_ge(o_ready, CHUNKS * (hf + 1))
                for e in range(HD):
                    sp.dma_start(CT[C * e:C * (e + 1), hf], On[:, hf, e, :]).then_inc(c_spread[hf], 16)
            for hf in range(HALVES):
                sp.wait_ge(y_ready, hf + 1)
                for rh in range(2):
                    sp.dma_start(token_view(out, hf, rh), y[64 * rh:64 * rh + 64, hf]).then_inc(s_out, 16)
            sp.wait_ge(s_out, 16 * 2 * HALVES)

        @block.gpsimd
        def _(pool):
            nc.gpsimd.memset(KS[32:64].rearrange("p h c n -> p (h c n)"), 0.0).then_inc(gap_zero, 1)
            pool.wait_ge(gap_zero, 1)
            nc.gpsimd.memset(VV[:, :, :, VC - 1:VC], 1.0).then_inc(gap_zero, 1)
            pool.wait_ge(gap_zero, 2)
            nc.gpsimd.memset(bias12[:, :], LN4096).then_inc(gap_zero, 1)
            pool.wait_ge(gap_zero, 3)
            for hf in range(HALVES):
                pool.wait_ge(v_spread[hf], 64)
                if hf:
                    pool.wait_ge(v_ordered, hf)
                nc.gpsimd.tensor_copy(VR[:, hf].rearrange("p (r c) -> p r c", c=C),
                                      VS[:, hf].rearrange("p c r -> p r c")).then_inc(v_ordered, 1)
            for t in range(HALVES * CHUNKS):
                pool.wait_ge(exps_ready, t + 1)
                if t == 0:
                    pool.wait_ge(v_ordered, HALVES)
                else:
                    pool.wait_ge(low_ready, t)
                if t >= 2:
                    pool.wait_ge(pT_psum, t - 1)
                nc.gpsimd.tensor_tensor(Pl[:, t % 2], P32[:, t % 2], Ph[:, t % 2], ALU.subtract)\
                    .then_inc(low_ready, 1)

        @block.scalar
        def _(act):
            def key_order(hf):
                act.wait_ge(k_spread[hf], spread_sizes())
                for b in range(2):
                    i = nc.scalar.copy(KR[:, hf, b].rearrange("p (r c) -> p r c", c=C),
                                       KS[:, hf, :, SKV * b:SKV * (b + 1)].rearrange("p c r -> p r c"))
                i.then_inc(k_ordered, 1)

            for hf in range(HALVES):
                act.wait_ge(xnT_psum, hf + 1)
                nc.scalar.copy(xnT[:, hf], ps[:, hf, :]).then_inc(xnT_ready, 1)
                act.wait_ge(v_psum, hf + 1)
                nc.scalar.copy(VT[:, hf], ps[:, 4 + hf, 0:KV]).then_inc(v_copied, 1)
            act.wait_ge(gap_zero, 3)
            key_order(0)
            for t in range(HALVES * CHUNKS):
                if t == CHUNKS // 2:
                    key_order(1)
                act.wait_ge(scores_used, t + 1)
                if t >= 2:
                    act.wait_ge(pT_psum, t - 1)
                    act.wait_ge(low_ready, t - 1)
                nc.scalar.activation(Ph[:, t % 2], Sm[:, t % 2], ACT.Exp, bias=bias12[:, 0:1], scale=SCALE)
                nc.scalar.activation(P32[:, t % 2], Sm[:, t % 2], ACT.Exp, bias=bias12[:, 0:1], scale=SCALE)\
                    .then_inc(exps_ready, 1)
                act.wait_ge(pT_psum, t + 1)
                if t >= 2:
                    act.wait_ge(pv_ready, t - 1)
                nc.scalar.copy(PT[:, t % 2, 0, :].bitcast(F32), ps[0:SKV, 4, :]).then_inc(pT_high, 1)
            for hf in range(HALVES):
                act.wait_ge(xn2T_psum, hf + 1)
                nc.scalar.copy(xn2T[:, hf], ps[:, 2 + hf, :]).then_inc(xn2T_ready, 1)
                act.wait_ge(logits_psum, hf + 1)
                if hf:
                    act.wait_ge(w3_ready, hf)
                nc.scalar.activation(ge[:, :, :], ps[:, 4, 0:RL * NE].rearrange("p (r e) -> p r e", e=NE),
                                     ACT.Exp, scale=-1.0).then_inc(gexp_ready, 1)
                act.wait_ge(w3T_psum, hf + 1)
                nc.scalar.copy(W3T[:, hf], ps[0:3 * NE, 5, 0:TOK // 2].bitcast(BF16)).then_inc(w3T_ready, 1)
            for hf in range(HALVES):
                for u in range(UNITS):
                    n = hf * UNITS + u
                    act.wait_ge(g_psum, n + 1)
                    if n >= 2:
                        act.wait_ge(h_ready, n - 1)
                    nc.scalar.activation(sg[:, n % 2], ps[:, n % 2, :], ACT.Silu).then_inc(silu_ready, 1)
                act.wait_ge(down_done, UNITS * (hf + 1))
                nc.scalar.copy(yT[:, :], ps[:, 6, :]).then_inc(yT_ready, 1)

        @block.vector
        def _(v):
            steps = [0]

            def link(ins):
                steps[0] += 1
                ins.then_inc(dve, 1)
                v.wait_ge(dve, steps[0])

            def layer_norm(src, done):
                for r in range(RL):
                    i = nc.vector.bn_stats(stats[:, r], src[:, r])
                link(i)
                for r in range(RL):
                    i = nc.vector.bn_aggr(mv[:, r], stats[:, r])
                link(i)
                link(nc.vector.tensor_scalar(lnv[:, :], mv[:, :, 1], EPS, None, ALU.add))
                link(nc.vector.tensor_scalar(lni[:, :], lnv[:, :].bitcast(I32), 1, None, ALU.logical_shift_right))
                link(nc.vector.tensor_scalar(lny[:, :].bitcast(I32), lni[:, :], -1.0, 1597463007.0, ALU.mult, ALU.add))
                for _ in range(3):
                    link(nc.vector.tensor_tensor(lnt[:, :], lny[:, :], lny[:, :], ALU.mult))
                    link(nc.vector.scalar_tensor_tensor(out=lnt[:, :], in0=lnt[:, :], scalar=-0.5, in1=lnv[:, :],
                                                        op0=ALU.mult, op1=ALU.mult))
                    link(nc.vector.scalar_tensor_tensor(out=lny[:, :], in0=lnt[:, :], scalar=1.5, in1=lny[:, :],
                                                        op0=ALU.add, op1=ALU.mult))
                for r in range(RL):
                    i = nc.vector.tensor_scalar(xn[:, r], src[:, r], mv[:, r, 0:1], lny[:, r:r + 1],
                                                ALU.subtract, ALU.mult)
                i.then_inc(done, 1)

            def split3(hi, mid, lo, src, tmp):
                link(nc.vector.tensor_copy(hi, src))
                link(nc.vector.tensor_tensor(tmp, src, hi, ALU.subtract))
                link(nc.vector.tensor_copy(mid, tmp))
                return nc.vector.tensor_tensor(lo, tmp, mid, ALU.subtract)

            for hf in range(HALVES):
                v.wait_ge(s_x[hf], 32)
                if hf:
                    v.wait_ge(xnT_psum, hf)
                layer_norm(x_sb[:, hf], xn_ready)
            for hf in range(HALVES):
                v.wait_ge(k_psum, hf + 1)
                split3(KT[:, hf, 0], KT[:, hf, 1], KT[:, hf, 2], ps[:, 2 + hf, 0:KV], res[:, 0:KV]).then_inc(k_split, 1)
                v.wait_ge(q_psum, hf + 1)

                src = ps[:, 6 + hf, :].rearrange("p (r g n) -> p g r n", r=RR, g=GROUPS)
                tmp = res[:, :].rearrange("p (g r n) -> p g r n", g=GROUPS, r=RR)
                part = [QT[:, hf, k].rearrange("p (g r n) -> p g r n", g=GROUPS, r=RR) for k in range(3)]
                split3(part[0], part[1], part[2], src, tmp).then_inc(q_split, 1)

            def gate(hf):
                v.wait_ge(gexp_ready, hf + 1)
                link(nc.vector.tensor_scalar(ge[:, :, :], ge[:, :, :], 1.0, None, ALU.add))
                link(nc.vector.reciprocal(gs[:, :, :], ge[:, :, :]))
                link(nc.vector.tensor_tensor(gsc[:, :, :], gs[:, :, :], gb[:, :].unsqueeze(1).broadcast_to([P, RL, NE]), ALU.add))
                hi = gsc[:, :, :].rearrange("p r (g k) -> p (r g) k", g=NG)
                lo = None
                n = NE // NG // 2
                k = 0
                while n >= 1:
                    a, b = hi[:, :, 0:n], hi[:, :, n:2 * n]
                    nh = th[:, 2 * (k % 2), 0:RL * NG * n].rearrange("p (q n) -> p q n", n=n)
                    nl = th[:, 2 * (k % 2) + 1, 0:RL * NG * n].rearrange("p (q n) -> p q n", n=n)
                    tl = th[:, 4, 0:RL * NG * n].rearrange("p (q n) -> p q n", n=n)
                    tm = th[:, 5, 0:RL * NG * n].rearrange("p (q n) -> p q n", n=n)
                    nc.vector.tensor_tensor(nh, a, b, ALU.max)
                    if lo is None:
                        link(nc.vector.tensor_tensor(nl, a, b, ALU.min))
                    else:
                        nc.vector.tensor_tensor(tl, a, b, ALU.min)
                        link(nc.vector.tensor_tensor(tm, lo[:, :, 0:n], lo[:, :, n:2 * n], ALU.max))
                        link(nc.vector.tensor_tensor(nl, tl, tm, ALU.max))
                    hi, lo = nh, nl
                    n //= 2
                    k += 1
                g3 = grp[:, :, :]
                link(nc.vector.tensor_tensor(g3, hi.rearrange("p (r g) n -> p r (g n)", r=RL),
                                             lo.rearrange("p (r g) n -> p r (g n)", r=RL), ALU.add))
                other = g3.unsqueeze(2).broadcast_to([P, RL, NG, NG])
                own = g3.unsqueeze(3).broadcast_to([P, RL, NG, NG])
                nc.vector.tensor_tensor(cmp[:, 0], other, own, ALU.is_gt)
                link(nc.vector.tensor_tensor(cmp[:, 1], other, own, ALU.is_equal))
                low4 = lower.rearrange("p (i j) -> p i j", i=NG).unsqueeze(1).broadcast_to([P, RL, NG, NG])
                link(nc.vector.tensor_tensor(cmp[:, 1], cmp[:, 1], low4, ALU.mult))
                link(nc.vector.tensor_tensor(cmp[:, 2], cmp[:, 0], cmp[:, 1], ALU.add))
                link(nc.vector.tensor_reduce(gcnt[:, :, :], cmp[:, 2], axis=AX.X, op=ALU.add))
                link(nc.vector.tensor_scalar(gcnt[:, :, :], gcnt[:, :, :], 1.5, None, ALU.is_lt))
                link(nc.vector.tensor_tensor(msk[:, :, :].rearrange("p r (g k) -> p r g k", g=NG),
                                             gsc[:, :, :].rearrange("p r (g k) -> p r g k", g=NG),
                                             gcnt[:, :, :].unsqueeze(3).broadcast_to([P, RL, NG, NE // NG]), ALU.mult))
                for r in range(RL):
                    i = nc.vector.max(top8[:, r], msk[:, r])
                link(i)
                for r in range(RL):
                    i = nc.vector.match_replace(out=repl[:, r], in_to_replace=top8[:, r], in_values=msk[:, r], imm_value=-3.0e38)
                link(i)
                link(nc.vector.tensor_tensor(repl[:, :, :], repl[:, :, :], msk[:, :, :], ALU.not_equal))
                link(nc.vector.tensor_tensor(wgt[:, :, :], gs[:, :, :], repl[:, :, :], ALU.mult))
                link(nc.vector.tensor_reduce(wsum[:, :], wgt[:, :, :], axis=AX.X, op=ALU.add))
                link(nc.vector.tensor_scalar(wsum[:, :], wsum[:, :], 1e-20, None, ALU.add))
                link(nc.vector.reciprocal(wsum[:, :], wsum[:, :]))
                link(nc.vector.tensor_scalar(wsum[:, :], wsum[:, :], ROUTED_SCALING, None, ALU.mult))
                link(nc.vector.tensor_tensor(wgt[:, :, :], wgt[:, :, :], wsum[:, :].unsqueeze(2).broadcast_to([P, RL, NE]), ALU.mult))
                if hf:
                    v.wait_ge(w3T_psum, hf)
                link(nc.vector.tensor_copy(w3[:, :, 0], wgt[:, :, :]))
                link(nc.vector.tensor_tensor(wres[:, :, :], wgt[:, :, :], w3[:, :, 0], ALU.subtract))
                link(nc.vector.tensor_copy(w3[:, :, 1], wres[:, :, :]))
                nc.vector.tensor_tensor(w3[:, :, 2], wres[:, :, :], w3[:, :, 1], ALU.subtract).then_inc(w3_ready, 1)

            def value_split(hf):
                v.wait_ge(vT_psum, hf + 1)
                src = ps[0:SKV, 7, :].rearrange("p (h b e) -> p h b e", h=NH, b=4)
                part = [VV[:, hf].rearrange("p (b h) k -> p h b k", h=NH)[:, :, :, HD * k:HD * (k + 1)] for k in range(3)]
                tmp = vres[:, :].rearrange("p (h b e) -> p h b e", h=NH, b=4)
                split3(part[0], part[1], part[2], src, tmp).then_inc(v_split, 1)

            def normalise(t):
                hf, k = t // CHUNKS, t % CHUNKS
                v.wait_ge(pv_ready, t + 1)
                if t:
                    v.wait_ge(o_ready, t)
                for g in range(GROUPS):
                    o = ps[:, 6 + t % 2, :].rearrange("p (g q) -> p g q", g=GROUPS)[:, g, 0:CH * 32]\
                        .rearrange("p (i k) -> p i k", k=32)
                    nc.vector.reciprocal(oden[:, g, 0:CH], o[:, :, VC - 1])
                    i = nc.vector.tensor_reduce(osum[:, g, 0:CH], o[:, :, 0:3 * HD].rearrange("p i (a e) -> p i e a", a=3),
                                                axis=AX.X, op=ALU.add)
                link(i)
                for g in range(GROUPS):
                    h0 = GH * g + CH * k
                    i = nc.vector.tensor_tensor(On[:, hf, :, h0:h0 + CH].rearrange("p e i -> p i e"), osum[:, g, 0:CH],
                                                oden[:, g, 0:CH].unsqueeze(2).broadcast_to([P, CH, HD]), ALU.mult)
                i.then_inc(o_ready, 1)

            value_split(0)
            NT = HALVES * CHUNKS
            for t in range(NT):
                if t == CHUNKS // 2 + 1:
                    value_split(1)
                v.wait_ge(scores_ready, t + 1)
                sc = ps[:, 2 * (t % 2):2 * (t % 2) + 2, 0:CH * SKV]
                link(nc.vector.tensor_reduce(mx[:, t % 2, :], sc.rearrange("p g (i j) -> p g i j", j=SKV), axis=AX.X, op=ALU.max))
                if t >= 2:
                    v.wait_ge(exps_ready, t - 1)
                for g in range(GROUPS):
                    i = nc.vector.tensor_tensor(Sm[:, t % 2, g], sc[:, g].rearrange("p (i j) -> p i j", j=SKV),
                                            mx[:, t % 2, CH * g:CH * (g + 1)].unsqueeze(2).broadcast_to([P, CH, SKV]),
                                            ALU.subtract)
                i.then_inc(scores_used, 1)
                v.wait_ge(pT_psum, t + 1)
                if t >= 2:
                    v.wait_ge(pv_ready, t - 1)
                nc.vector.tensor_copy(PT[:, t % 2, 1, :].bitcast(F32), ps[0:SKV, 5, :]).then_inc(pT_low, 1)
                if t >= 1:
                    normalise(t - 1)
            normalise(NT - 1)
            for hf in range(HALVES):
                v.wait_ge(proj_psum, hf + 1)
                link(nc.vector.tensor_tensor(x1[:, hf].rearrange("p l d -> p (l d)"),
                                             x_sb[:, hf].rearrange("p l d -> p (l d)"), ps[:, hf, :], ALU.add))
                if hf:
                    v.wait_ge(xn2T_psum, hf)
                layer_norm(x1[:, hf], xn2_ready)
            v.wait_ge(s_gw, 48)
            for hf in range(HALVES):
                gate(hf)
            for hf in range(HALVES):
                for u in range(UNITS):
                    n = hf * UNITS + u
                    v.wait_ge(silu_ready, n + 1)
                    v.wait_ge(u_psum, n + 1)
                    if n >= 2:
                        v.wait_ge(down_done, n - 1)
                    if u < PAIRS:
                        link(nc.vector.tensor_tensor(h1[:, n % 2], sg[:, n % 2], ps[:, 2 + n % 2, :], ALU.mult))
                        v.wait_ge(wb_psum, hf * PAIRS + u + 1)
                        nc.vector.tensor_tensor(hw[:, n % 2], h1[:, n % 2], ps[:, 4 + n % 2, :], ALU.mult).then_inc(h_ready, 1)
                    else:
                        nc.vector.tensor_tensor(hw[:, n % 2], sg[:, n % 2], ps[:, 2 + n % 2, :], ALU.mult).then_inc(h_ready, 1)
                v.wait_ge(y_psum, hf + 1)
                nc.vector.tensor_tensor(y[:, hf].rearrange("p l d -> p (l d)"),
                                        x1[:, hf].rearrange("p l d -> p (l d)"), ps[:, 7, :], ALU.add).then_inc(y_ready, 1)

        @block.tensor
        def _(pe):
            mm = nc.tensor.matmul
            pe.wait_ge(s_cf, 16)
            pe.wait_ge(s_ctx, 32)
            for hf in range(HALVES):
                mm(ps[:, 2 + hf, 0:KV], wat[:, 1], ctx_sb[:, hf], start=True, stop=True).then_inc(k_psum, 1)
                mm(ps[:, 4 + hf, 0:KV], wat[:, 2], ctx_sb[:, hf], start=True, stop=True).then_inc(v_psum, 1)
            for hf in range(HALVES):
                pe.wait_ge(xn_ready, hf + 1)
                for r in range(RL):
                    i = nc.tensor.transpose(ps[:, hf, P * r:P * (r + 1)], xn[:, r], identf)
                i.then_inc(xnT_psum, 1)
                pe.wait_ge(xnT_ready, hf + 1)
                mm(ps[:, 6 + hf, :], wat[:, 0], xnT[:, hf], start=True, stop=True).then_inc(q_psum, 1)
            pe.wait_ge(s_cb, 32)

            def values(hf):
                pe.wait_ge(v_ordered, hf + 1)
                if hf == 0:
                    pe.wait_ge(q_split, 2)
                else:
                    pe.wait_ge(o_ready, CHUNKS // 2)
                for h in range(NH):
                    i = nc.tensor.transpose(ps[0:SKV, 7, 32 * h:32 * h + 32], VR[:, hf, SKV * h:SKV * (h + 1)],
                                            identf[0:4 * HD, 0:4 * HD])
                i.then_inc(vT_psum, 1)

            def scores(t):
                hf, k = t // CHUNKS, t % CHUNKS
                if t >= 2:
                    pe.wait_ge(scores_used, t - 1)
                if k == 0:
                    pe.wait_ge(q_spread[hf], spread_sizes())
                    pe.wait_ge(k_ordered, hf + 1)
                for g in range(GROUPS):
                    mm(ps[:, 2 * (t % 2) + g, 0:CH * SKV], identb, maskneg, start=True, stop=False)
                for i in range(CH):
                    for g in range(GROUPS):
                        n = CH * k + i
                        h = n % NH
                        last = mm(ps[:, 2 * (t % 2) + g, SKV * i:SKV * (i + 1)],
                                  QS[GP * g:GP * g + ROWS, hf, :, n],
                                  KR[GP * g:GP * g + ROWS, hf, n // NH, SKV * h:SKV * (h + 1)],
                                  start=False, stop=(i == CH - 1))
                last.then_inc(scores_ready, 1)

            def turn(t):
                pe.wait_ge(low_ready, t + 1)
                if t >= 1:
                    pe.wait_ge(pT_high, t)
                    pe.wait_ge(pT_low, t)
                for part, src in ((0, Ph), (1, Pl)):
                    for g in range(GROUPS):
                        for i in range(CH):
                            q = CH * g + i
                            last = nc.tensor.transpose(ps[0:SKV, 4 + part, 64 * q:64 * (q + 1)].bitcast(F16),
                                                       src[:, t % 2, g, i, :], ch[:, :])
                last.then_inc(pT_psum, 1)

            def weigh(t):
                hf, k = t // CHUNKS, t % CHUNKS
                pe.wait_ge(pT_high, t + 1)
                pe.wait_ge(pT_low, t + 1)
                pe.wait_ge(v_split, 1 + (t > CHUNKS // 2))
                if t >= 2:
                    pe.wait_ge(o_ready, t - 1)
                for g in range(GROUPS):
                    for i in range(CH):
                        q = CH * g + i
                        n = GH * g + CH * k + i
                        for part in range(2):
                            last = mm(ps[:, 6 + t % 2, 256 * g + 32 * i:256 * g + 32 * i + VC],
                                      PT[:, t % 2, part, P * q:P * (q + 1)], VV[:, hf, n, :],
                                      start=(part == 0), stop=(part == 1))
                last.then_inc(pv_ready, 1)

            NT = HALVES * CHUNKS
            values(0)
            scores(0)
            for t in range(NT):
                if t + 1 < NT:
                    scores(t + 1)
                turn(t)
                weigh(t)
                if t == CHUNKS // 2:
                    values(1)
            for hf in range(HALVES):
                pe.wait_ge(c_spread[hf], 16 * HD)
                if hf == 0:
                    pe.wait_ge(scores_used, NT)
                for r in range(RL):
                    last = mm(ps[:, hf, P * r:P * (r + 1)],
                              CT[:, hf, 2 * r:2 * r + 2, :].rearrange("p r n -> p (r n)"), wat[:, 3],
                              start=True, stop=True)
                last.then_inc(proj_psum, 1)
            for hf in range(HALVES):
                pe.wait_ge(xn2_ready, hf + 1)
                for r in range(RL):
                    last = nc.tensor.transpose(ps[:, 2 + hf, P * r:P * (r + 1)], xn[:, r], identf)
                last.then_inc(xn2T_psum, 1)
            pe.wait_ge(s_gw, 48)
            for hf in range(HALVES):
                pe.wait_ge(xn2T_ready, hf + 1)
                if hf:
                    pe.wait_ge(gexp_ready, hf)
                for r in range(RL):
                    last = mm(ps[:, 4, NE * r:NE * (r + 1)], xn2T[:, hf, P * r:P * (r + 1)], gw[:, :],
                              start=True, stop=True)
                last.then_inc(logits_psum, 1)
                pe.wait_ge(w3_ready, hf + 1)
                if hf:
                    pe.wait_ge(w3T_ready, hf)
                for r in range(RL):
                    last = nc.tensor.transpose(ps[0:3 * NE, 5, 64 * r:64 * (r + 1)].bitcast(BF16),
                                               w3[:, r].rearrange("p a e -> p (a e)"), identb)
                last.then_inc(w3T_psum, 1)
            pe.wait_ge(s_eg, 48)
            pe.wait_ge(w3T_ready, HALVES)

            def up(n):
                hf, u = n // UNITS, n % UNITS
                if n >= 2:
                    pe.wait_ge(silu_ready, n - 1)
                mm(ps[:, n % 2, :], egs[:, u], xn2T[:, hf], start=True, stop=True).then_inc(g_psum, 1)
                if n >= 2:
                    pe.wait_ge(h_ready, n - 1)
                mm(ps[:, 2 + n % 2, :], eus[:, u], xn2T[:, hf], start=True, stop=True).then_inc(u_psum, 1)
                if u < PAIRS:
                    mm(ps[:, 4 + n % 2, :], sel[:, u], W3T[:, hf], start=True, stop=True).then_inc(wb_psum, 1)

            def down(n):
                hf, u = n // UNITS, n % UNITS
                pe.wait_ge(h_ready, n + 1)
                if u == 0 and hf:
                    pe.wait_ge(yT_ready, hf)
                mm(ps[:, 6, :], eds[:, u], hw[:, n % 2], start=(u == 0), stop=(u == UNITS - 1)).then_inc(down_done, 1)
                if u == UNITS - 1:
                    pe.wait_ge(yT_ready, hf + 1)
                    if hf:
                        pe.wait_ge(y_ready, hf)
                    for r in range(RL):
                        last = nc.tensor.transpose(ps[:, 7, P * r:P * (r + 1)], yT[:, P * r:P * (r + 1)], identf)
                    last.then_inc(y_psum, 1)

            up(0)
            for n in range(HALVES * UNITS):
                if n + 1 < HALVES * UNITS:
                    up(n + 1)
                down(n)


def kernel(x, ctx_1024, L0_xattn_wq, L0_xattn_wk, L0_xattn_wv, L0_xattn_wproj, L0_ffn_gate_w, L0_ffn_gate_bias,
           L0_ffn_expert_gate, L0_ffn_expert_up, L0_ffn_expert_down, L0_ffn_shared_gate, L0_ffn_shared_up,
           L0_ffn_shared_down):
    import numpy as np
    import ml_dtypes
    import concourse.bacc as bacc
    from concourse.bass_utils import run_bass_kernel_spmd

    def a(t):
        return np.ascontiguousarray(t)

    x = a(x)
    ctxT = a(np.asarray(ctx_1024).reshape(B * SKV, D).T).reshape(D, HALVES, KV)

    def lane_first(t):
        return t.reshape(D, C, HD).transpose(0, 2, 1).reshape(D, D)

    wattn = [lane_first(np.asarray(w).T) for w in (L0_xattn_wq, L0_xattn_wk, L0_xattn_wv)]
    wattn = a(np.stack(wattn + [lane_first(np.asarray(L0_xattn_wproj)).T], 1))
    gwT = a(np.asarray(L0_ffn_gate_w).T)

    def rows(e, s):
        t = np.concatenate([np.asarray(e).reshape(-1, D), np.asarray(s)], 0)
        return a(t.T.reshape(D, UNITS, P))

    eg = rows(L0_ffn_expert_gate, L0_ffn_shared_gate)
    eu = rows(L0_ffn_expert_up, L0_ffn_shared_up)
    dn = np.concatenate([np.asarray(L0_ffn_expert_down).transpose(0, 2, 1).reshape(-1, D),
                         np.asarray(L0_ffn_shared_down).T], 0)
    ed = a(dn.reshape(UNITS, P, D).transpose(1, 0, 2))

    p = np.arange(P)
    r = p % RR
    query = C * (RL * (r % 2) + r // 2) + p // RR
    neg = np.where(np.arange(SKV)[None, :] > query[:, None], -1e30, 0.0)
    cbf16 = np.concatenate([np.eye(P)] + [neg] * CH, 1).astype(ml_dtypes.bfloat16)
    low = np.tril(np.ones((NG, NG)), -1).reshape(1, -1).repeat(P, 0)
    cf32 = np.concatenate([np.eye(P), low], 1).astype(np.float32)
    cf16 = np.eye(P).astype(np.float16)
    expert = 2 * np.arange(PAIRS)[:, None] + np.arange(P)[None, :] // 64
    csel = np.tile(np.arange(NE)[:, None, None] == expert[None], (3, 1, 1)).astype(ml_dtypes.bfloat16)

    arrays = {"x": x, "ctxT": ctxT, "wattn": wattn, "gwT": gwT, "gbias": a(L0_ffn_gate_bias), "eg": eg, "eu": eu,
              "ed": ed, "cf32": cf32, "cbf16": cbf16, "cf16": cf16, "csel": csel}
    nc = bacc.Bacc("TRN2", target_bir_lowering=False, num_devices=1)
    aps = [nc.dram_tensor(k, t.shape, mybir.dt.from_np(t.dtype), kind="ExternalInput").ap() for k, t in arrays.items()]
    out = nc.dram_tensor("out", (B, S, D), F32, kind="ExternalOutput").ap()
    block_kernel(nc, *aps, out)
    r = run_bass_kernel_spmd(nc, [arrays], core_ids=[0])
    return r.results[0]["out"]
```

```python
from contextlib import ExitStack

import concourse.bass as bass
from concourse import mybir

ALU = mybir.AluOpType
ACT = mybir.ActivationFunctionType
AX = mybir.AxisListType
F32 = mybir.dt.float32
I32 = mybir.dt.int32
BF16 = mybir.dt.bfloat16
F16 = mybir.dt.float16

P = 128
D = 128
B, S, SKV = 8, 128, 77
NH, HD = 16, 8
HALVES = 2
BH = B // HALVES * NH
TOK = B // HALVES * S
KV = B // HALVES * SKV
RR = S // NH
RL = TOK // P
C = D // HD
NKEY = SKV * C
CH = 4
CB = 2
CHUNKS = BH // (CH * CB)
NT = HALVES * CHUNKS
BUF = 4
NE = 32
NG = 4
TOPK = 8
PAIRS = NE // 2
UNITS = PAIRS + 1
ROUTED_SCALING = 2.5
EPS = 1e-5
XSCALE = 4096.0
WSCALE = 8192.0
SCALE = float(HD) ** -0.5
LN4096 = 8.317766166719343
PARTS = 3
ROWS = PARTS * PARTS * HD
VC = 3 * HD + 1


def block_kernel(nc, x, ctxT, wattn, gwT, gbias, eg, eu, ed, cf32, cbf16, cf16, csel, out):
    kd = nc.dram_tensor("kd", (PARTS, HD, C, HALVES * KV), BF16).ap()
    vd = nc.dram_tensor("vd", (B, HD, C, SKV), F32).ap()
    qd = nc.dram_tensor("qd", (HALVES, PARTS, HD, C, TOK), BF16).ap()
    od = nc.dram_tensor("od", (HALVES, C, RR, HD, BH), F32).ap()

    with ExitStack() as ctx:
        def sb(name, shape, dt=F32):
            return ctx.enter_context(nc.sbuf_tensor(name, shape, dt))

        def sem(name):
            return ctx.enter_context(nc.semaphore(name))

        x_sb = sb("x_sb", [P, HALVES, RL, D])
        ctx_sb = sb("ctx_sb", [P, HALVES, KV])
        wat = sb("wat", [P, 4, D])
        gw = sb("gw", [P, NE])
        gb = sb("gb", [P, NE])
        egu = sb("egu", [P, 2, UNITS, P])
        eds = sb("eds", [P, UNITS, P])
        VS = eds[0:B * HD].rearrange("p u m -> p (u m)")[:, 0:NKEY].rearrange("p (c n) -> p c n", c=C)
        cf = sb("cf", [P, P + NG * NG])
        cb = sb("cb", [P, P + CH * SKV], BF16)
        ch = sb("ch", [P, P], F16)
        sel = sb("sel", [3 * NE, PAIRS, P], BF16)
        identf = cf[:, 0:P]
        lower = cf[:, P:P + NG * NG]
        identb = cb[:, 0:P]
        maskneg = cb[:, P:P + CH * SKV]

        wmax = sb("wmax", [P, 2])
        wall = sb("wall", [P, 2])
        wpow = sb("wpow", [P, 2])
        wfac = sb("wfac", [P, 2])
        winv = sb("winv", [P, 2])
        wh = sb("wh", [P, 2, UNITS * P], F16)
        wl = sb("wl", [P, 2, UNITS * P], F16)

        wsc = egu[:, :, :, :].rearrange("p k u m -> p k (u m)")

        stats = sb("stats", [P, HALVES * RL, 6])
        mv = sb("mv", [P, HALVES * RL, 2])
        lnv = sb("lnv", [P, HALVES * RL])
        lni = sb("lni", [P, HALVES * RL], I32)
        lny = sb("lny", [P, HALVES * RL])
        lnt = sb("lnt", [P, HALVES * RL])
        xn = sb("xn", [P, HALVES * RL, D])
        xn2 = xn[:, :, :].rearrange("p (f r) d -> p f r d", f=HALVES)
        y = xn2
        xnT = sb("xnT", [P, HALVES, TOK])
        xn2T = xnT
        xh = sb("xh", [P, HALVES, TOK], F16)
        xl = sb("xl", [P, HALVES, TOK], F16)

        QT = sb("QT", [P, HALVES, PARTS, TOK], BF16)
        KT = sb("KT", [P, PARTS, HALVES * KV], BF16)
        VT = sb("VT", [P, HALVES * KV])
        res = sb("res", [P, HALVES * KV])
        QS = sb("QS", [ROWS, HALVES, C * RR, BH], BF16)
        early = sb("early", [P, 2, BUF, CB, CH, SKV])
        Sm, P32 = early[:, 0], early[:, 1]
        KS = early[0:ROWS].rearrange("p a b g i j -> p (a b g i j)").bitcast(BF16).rearrange("p (c n) -> p c n", c=C)
        KR = sb("KR", [ROWS, B, NKEY], BF16)
        VR = sb("VR", [B * HD, NKEY])
        VV = sb("VV", [SKV, B * NH, VC], BF16)
        mx = sb("mx", [P, BUF, CB * CH])
        Ph = sb("Ph", [P, BUF, CB, CH, SKV], F16)
        Pl = sb("Pl", [P, BUF, CB, CH, SKV], F16)
        PT = sb("PT", [SKV, 2, 2, CB * CH * P], F16)
        osum = sb("osum", [P, 2, CB * CH, HD])
        oden = sb("oden", [P, 2, CB * CH])
        On = QT[:, :].rearrange("p f a n -> p (f a n)").bitcast(F32)[:, 0:HALVES * HD * BH]\
            .rearrange("p (f e n) -> p f e n", f=HALVES, e=HD)
        CT = sb("CT", [P, HALVES, RR, BH])
        x1 = sb("x1", [P, HALVES, RL, D])
        bias12 = sb("bias12", [P, 1])

        ge = sb("ge", [P, RL, NE])
        gs = sb("gs", [P, RL, NE])
        gsc = sb("gsc", [P, RL, NE])
        th = sb("th", [P, 6, RL * NG * 4])
        grp = sb("grp", [P, RL, NG])
        cmp = sb("cmp", [P, 3, RL, NG, NG])
        gcnt = sb("gcnt", [P, RL, NG])
        msk = sb("msk", [P, RL, NE])
        top8 = sb("top8", [P, RL, 8])
        repl = sb("repl", [P, RL, NE])
        wgt = sb("wgt", [P, RL, NE])
        wsum = sb("wsum", [P, RL])
        w3 = sb("w3", [P, RL, 3, NE], BF16)
        wres = sb("wres", [P, RL, NE])
        W3T = sb("W3T", [3 * NE, HALVES, TOK], BF16)

        flat = egu[:, :, :, :].rearrange("p k u m -> p (k u m)")
        sg, h1, hw = (flat[:, 2 * TOK * i:2 * TOK * (i + 1)].rearrange("p (b n) -> p b n", b=2) for i in range(3))
        yT = flat[:, 6 * TOK:7 * TOK]

        ps = ctx.enter_context(nc.psum_tensor("ps", [P, 8, 512], F32))
        MISC = 7

        s_cf = sem("s_cf")
        s_x = sem("s_x")
        s_ctx = sem("s_ctx")
        s_gw = sem("s_gw")
        s_egu = sem("s_egu")
        s_ed = sem("s_ed")
        s_cb = sem("s_cb")
        consts_set = sem("consts_set")
        dve = sem("dve")
        wmax_ready = sem("wmax_ready")
        wall_ready = sem("wall_ready")
        wfac_ready = sem("wfac_ready")
        whigh_ready = sem("whigh_ready")
        wlow_ready = sem("wlow_ready")
        xn_ready = sem("xn_ready")
        xnT_psum = sem("xnT_psum")
        xnT_ready = sem("xnT_ready")
        k_psum = sem("k_psum")
        v_psum = sem("v_psum")
        q_psum = sem("q_psum")
        k_split = sem("k_split")
        v_copied = sem("v_copied")
        q_split = sem("q_split")
        k_dram = sem("k_dram")
        v_dram = sem("v_dram")
        q_dram = sem("q_dram")
        o_dram = sem("o_dram")
        k_spread = sem("k_spread")
        v_spread = sem("v_spread")
        q_spread = [sem(f"q_spread{i}") for i in range(HALVES)]
        c_spread = [sem(f"c_spread{i}") for i in range(HALVES)]
        k_ordered = sem("k_ordered")
        v_ordered = sem("v_ordered")
        vT_psum = sem("vT_psum")
        v_split = sem("v_split")
        scores_ready = sem("scores_ready")
        scores_used = sem("scores_used")
        exps_ready = sem("exps_ready")
        low_ready = sem("low_ready")
        pT_psum = sem("pT_psum")
        pT_high = sem("pT_high")
        pT_low = sem("pT_low")
        pv_ready = sem("pv_ready")
        o_ready = sem("o_ready")
        proj_psum = sem("proj_psum")
        xn2_ready = sem("xn2_ready")
        xn2T_psum = sem("xn2T_psum")
        xn2T_ready = sem("xn2T_ready")
        xlow_ready = sem("xlow_ready")
        logits_psum = sem("logits_psum")
        gexp_ready = sem("gexp_ready")
        w3_ready = sem("w3_ready")
        w3T_psum = sem("w3T_psum")
        w3T_ready = sem("w3T_ready")
        g_psum = sem("g_psum")
        u_psum = sem("u_psum")
        wb_psum = sem("wb_psum")
        silu_ready = sem("silu_ready")
        h_ready = sem("h_ready")
        down_done = sem("down_done")
        yT_ready = sem("yT_ready")
        y_psum = sem("y_psum")
        y_ready = sem("y_ready")
        s_out = sem("s_out")

        def token_view(t, hf, rh):
            v = t.rearrange("(f n) s d -> f (n s) d", f=HALVES)[hf]
            return v.rearrange("(a h l) d -> h a l d", h=2, l=RL)[rh]

        POST = {0: dict(spread=9, proj=11, norm=11, turn=12, low=13, logits=13, gate=14),
                1: dict(spread=1, proj=3, norm=3, turn=5, low=6, logits=6, gate=7, w3=11)}

        block = ctx.enter_context(nc.Block())

        @block.sync
        def _(sp):
            for hf in range(HALVES):
                for rh in range(2):
                    sp.dma_start(x_sb[64 * rh:64 * rh + 64, hf], token_view(x, hf, rh)).then_inc(s_x, 16)
            sp.dma_start(ctx_sb[:, :, :], ctxT).then_inc(s_ctx, 16)
            sp.dma_start(wat[:, :, :], wattn).then_inc(s_ctx, 16)
            sp.dma_start(cf[:, :], cf32).then_inc(s_cf, 16)
            sp.wait_ge(v_copied, 1)
            sp.dma_start(vd.rearrange("b e c n -> (e c) b n"), VT[:, :]).then_inc(v_dram, 16)
            sp.wait_ge(k_split, 1)
            sp.dma_start(kd.rearrange("a e c n -> (e c) a n"), KT[:, :, :]).then_inc(k_dram, 16)
            sp.wait_ge(v_dram, 16)
            sp.dma_start(VS, vd.rearrange("b e c n -> (b e) c n")).then_inc(v_spread, 16)
            sp.wait_ge(k_dram, 16)
            for i in range(PARTS):
                sp.dma_start(KS[PARTS * HD * i:PARTS * HD * (i + 1)].rearrange("p c n -> p (c n)"),
                             kd.rearrange("a e c n -> e a (c n)")).then_inc(k_spread, 16)
            for hf in range(HALVES):
                sp.wait_ge(q_split, hf + 1)
                sp.dma_start(qd[hf].rearrange("a e c n -> (e c) a n"), QT[:, hf]).then_inc(q_dram, 16)
                sp.wait_ge(q_dram, 16 * (hf + 1))
                sp.dma_start(QS[:, hf].rearrange("p c n -> p (c n)"),
                             qd[hf].rearrange("a e c n -> (a e) (c n)").unsqueeze(1)
                             .broadcast_to([PARTS * HD, PARTS, C * TOK])).then_inc(q_spread[hf], 16)
                if hf == 0:
                    sp.dma_start(cb[:, :], cbf16).then_inc(s_cb, 16)
                    sp.dma_start(ch[:, :], cf16).then_inc(s_cb, 16)
            for k, src in ((0, eg), (1, eu)):
                sp.dma_start(egu[:, k], src).then_inc(s_egu, 16)
            sp.dma_start(gw[:, :], gwT).then_inc(s_gw, 16)
            sp.dma_start(gb[:, :], gbias.partition_broadcast(P)).then_inc(s_gw, 16)
            sp.dma_start(sel[:, :, :], csel).then_inc(s_gw, 16)
            sp.wait_ge(v_ordered, 1)
            sp.dma_start(eds[:, :, :], ed).then_inc(s_ed, 16)
            for hf in range(HALVES):
                sp.wait_ge(o_ready, CHUNKS * (hf + 1))
                sp.dma_start(od[hf].rearrange("c r e n -> (c r) e n"), On[:, hf]).then_inc(o_dram, 16)
                sp.wait_ge(o_dram, 16 * (hf + 1))
                sp.dma_start(CT[:, hf], od[hf].rearrange("c r e n -> e c r n")).then_inc(c_spread[hf], 16)
            for hf in range(HALVES):
                sp.wait_ge(y_ready, hf + 1)
                for rh in range(2):
                    sp.dma_start(token_view(out, hf, rh), y[64 * rh:64 * rh + 64, hf]).then_inc(s_out, 16)
            sp.wait_ge(s_out, 16 * 2 * HALVES)

        @block.gpsimd
        def _(pool):
            nc.gpsimd.memset(bias12[:, :], LN4096).then_inc(consts_set, 1)
            pool.wait_ge(consts_set, 1)
            nc.gpsimd.memset(VV[:, :, VC - 1:VC], 1.0).then_inc(consts_set, 1)
            for t in range(NT):
                pool.wait_ge(exps_ready, t + 1)
                if t == 0:
                    pool.wait_ge(consts_set, 2)
                else:
                    pool.wait_ge(low_ready, t)
                if t >= BUF:
                    pool.wait_ge(pT_psum, t - BUF + 1)
                nc.gpsimd.tensor_tensor(Pl[:, t % BUF], P32[:, t % BUF], Ph[:, t % BUF], ALU.subtract)\
                    .then_inc(low_ready, 1)
                if t == 2:
                    pool.wait_ge(wmax_ready, 1)
                    pool.wait_ge(low_ready, t + 1)
                    nc.gpsimd.partition_all_reduce(wall[:, :], wmax[:, :], P, bass.bass_isa.ReduceOp.max)\
                        .then_inc(wall_ready, 1)
                    pool.wait_ge(wall_ready, 1)
                if 5 <= t < 5 + 2 * 5:
                    k, f = (t - 5) // 5, (t - 5) % 5
                    a, b = f * UNITS * P // 5, min((f + 1) * UNITS * P // 5, UNITS * P)
                    pool.wait_ge(whigh_ready, k + 1)
                    pool.wait_ge(low_ready, t + 1)
                    nc.gpsimd.tensor_tensor(wl[:, k, a:b], wsc[:, k, a:b], wh[:, k, a:b], ALU.subtract)\
                        .then_inc(wlow_ready, 1)
                    pool.wait_ge(wlow_ready, t - 4)

        @block.scalar
        def _(act):
            def key_order(batches):
                for b in batches:
                    i = nc.scalar.copy(KR[:, b].rearrange("p (r c) -> p r c", c=C),
                                       KS[:, :, SKV * b:SKV * (b + 1)].rearrange("p c r -> p r c"))
                i.then_inc(k_ordered, 1)

            def exps(t):
                act.wait_ge(scores_used, t + 1)
                if t >= BUF:
                    act.wait_ge(pT_psum, t - BUF + 1)
                    act.wait_ge(low_ready, t - BUF + 1)
                b = t % BUF
                nc.scalar.activation(Ph[:, b], Sm[:, b], ACT.Exp, bias=bias12[:, 0:1], scale=SCALE)
                nc.scalar.activation(P32[:, b], Sm[:, b], ACT.Exp, bias=bias12[:, 0:1], scale=SCALE)\
                    .then_inc(exps_ready, 1)

            def weights_high(k):
                act.wait_ge(wfac_ready, 1)
                nc.scalar.activation(wh[:, k, :], wsc[:, k, :], ACT.Copy, scale=wfac[:, k:k + 1])
                nc.scalar.activation(wsc[:, k, :], wsc[:, k, :], ACT.Copy, scale=wfac[:, k:k + 1]).then_inc(whigh_ready, 1)

            def post(hf, at):
                step = POST[hf]
                if at == step["turn"]:
                    act.wait_ge(xn2T_psum, hf + 1)
                    nc.scalar.copy(xn2T[:, hf], ps[:, MISC, :])
                    nc.scalar.mul(xh[:, hf], ps[:, MISC, :], XSCALE).then_inc(xn2T_ready, 1)
                if at == step["logits"]:
                    act.wait_ge(logits_psum, hf + 1)
                    if hf:
                        act.wait_ge(w3_ready, hf)
                    nc.scalar.activation(ge[:, :, :], ps[:, MISC, 0:RL * NE].rearrange("p (r e) -> p r e", e=NE),
                                         ACT.Exp, scale=-1.0).then_inc(gexp_ready, 1)
                if at == step.get("w3", NT):
                    act.wait_ge(w3T_psum, hf + 1)
                    nc.scalar.copy(W3T[:, hf], ps[0:3 * NE, MISC, 0:TOK // 2].bitcast(BF16)).then_inc(w3T_ready, 1)

            act.wait_ge(v_psum, 1)
            nc.scalar.copy(VT[:, :].rearrange("p (f n) -> p f n", f=HALVES), ps[:, 4:6, 0:KV]).then_inc(v_copied, 1)
            for hf in range(HALVES):
                act.wait_ge(xnT_psum, hf + 1)
                nc.scalar.copy(xnT[:, hf], ps[:, hf, :]).then_inc(xnT_ready, 1)
            act.wait_ge(v_spread, 16)
            nc.scalar.copy(VR[:, :].rearrange("p (r c) -> p r c", c=C), VS.rearrange("p c r -> p r c")).then_inc(v_ordered, 1)
            act.wait_ge(k_spread, 16 * PARTS)
            key_order(range(1, B, 2))
            act.wait_ge(consts_set, 1)
            exps(0)
            for t in range(NT):
                if t + 1 < NT:
                    exps(t + 1)
                act.wait_ge(pT_psum, t + 1)
                if t >= 2:
                    act.wait_ge(pv_ready, t - 1)
                nc.scalar.copy(PT[:, t % 2, 0, :].bitcast(F32), ps[0:SKV, 4, :]).then_inc(pT_high, 1)
                if t in (3, 5):
                    weights_high((t - 3) // 2)
                post(0, t)
            post(0, NT)
            for hf in range(HALVES):
                for u in range(UNITS):
                    n = hf * UNITS + u
                    act.wait_ge(g_psum, n + 1)
                    if n >= 2:
                        act.wait_ge(h_ready, n - 1)
                    nc.scalar.activation(sg[:, n % 2], ps[:, n % 2, :], ACT.Silu, scale=winv[:, 0:1]).then_inc(silu_ready, 1)
                    if hf == 0:
                        post(1, u)
                act.wait_ge(down_done, UNITS * (hf + 1))
                nc.scalar.copy(yT[:, :], ps[:, 6, :]).then_inc(yT_ready, 1)

        @block.vector
        def _(v):
            steps = [0]

            def link(ins):
                steps[0] += 1
                ins.then_inc(dve, 1)
                v.wait_ge(dve, steps[0])

            def row_stats(tiles):
                n = len(tiles)
                for r in range(n):
                    i = nc.vector.bn_stats(stats[:, r], tiles[r])
                link(i)
                for r in range(n):
                    i = nc.vector.bn_aggr(mv[:, r], stats[:, r])
                link(i)
                var, guess, y, t = lnv[:, 0:n], lni[:, 0:n], lny[:, 0:n], lnt[:, 0:n]
                link(nc.vector.tensor_scalar(var, mv[:, 0:n, 1], EPS, None, ALU.add))
                link(nc.vector.tensor_scalar(guess, var.bitcast(I32), 1, None, ALU.logical_shift_right))
                link(nc.vector.tensor_scalar(y.bitcast(I32), guess, -1.0, 1597463007.0, ALU.mult, ALU.add))
                for _ in range(3):
                    link(nc.vector.tensor_tensor(t, y, y, ALU.mult))
                    link(nc.vector.scalar_tensor_tensor(out=t, in0=t, scalar=-0.5, in1=var, op0=ALU.mult, op1=ALU.mult))
                    link(nc.vector.scalar_tensor_tensor(out=y, in0=t, scalar=1.5, in1=y, op0=ALU.add, op1=ALU.mult))

            def normalise_row(dst, src, r):
                return nc.vector.tensor_scalar(dst, src, mv[:, r, 0:1], lny[:, r:r + 1], ALU.subtract, ALU.mult)

            def split3(hi, mid, lo, src, tmp):
                link(nc.vector.tensor_copy(hi, src))
                link(nc.vector.tensor_tensor(tmp, src, hi, ALU.subtract))
                link(nc.vector.tensor_copy(mid, tmp))
                return nc.vector.tensor_tensor(lo, tmp, mid, ALU.subtract)

            def keys_split():
                v.wait_ge(k_psum, 1)
                part = [KT[:, k].rearrange("p (f n) -> p f n", f=HALVES) for k in range(3)]
                tmp = res[:, 0:HALVES * KV].rearrange("p (f n) -> p f n", f=HALVES)
                split3(part[0], part[1], part[2], ps[:, 2:4, 0:KV], tmp).then_inc(k_split, 1)
                v.wait_ge(k_split, 1)

            def values_split(bank):
                src = ps[0:SKV, 4 + bank, :].rearrange("p (h b e) -> p h b e", h=NH // 2, b=B)
                part = [VV[:, :].rearrange("p (b h) k -> p h b k", h=NH)[:, NH // 2 * bank:NH // 2 * (bank + 1), :, HD * k:HD * (k + 1)]
                        for k in range(3)]
                tmp = res[0:SKV, 0:TOK].rearrange("p (h b e) -> p h b e", h=NH // 2, b=B)
                split3(part[0], part[1], part[2], src, tmp).then_inc(v_split, 1)
                v.wait_ge(v_split, bank + 1)

            def key_order(batches):
                for b in batches:
                    i = nc.vector.tensor_copy(KR[:, b].rearrange("p (r c) -> p r c", c=C),
                                              KS[:, :, SKV * b:SKV * (b + 1)].rearrange("p c r -> p r c"))
                i.then_inc(k_ordered, 1)

            def shift(t):
                v.wait_ge(scores_ready, t + 1)
                if t >= BUF:
                    v.wait_ge(exps_ready, t - BUF + 1)
                sc = ps[:, 2 * (t % 2):2 * (t % 2) + 2, 0:CH * SKV].rearrange("p g (i j) -> p g i j", j=SKV)
                m = mx[:, t % BUF].rearrange("p (g i) -> p g i", g=CB)
                link(nc.vector.tensor_reduce(m, sc, axis=AX.X, op=ALU.max))
                nc.vector.tensor_tensor(Sm[:, t % BUF], sc, m.unsqueeze(3).broadcast_to([P, CB, CH, SKV]),
                                        ALU.subtract).then_inc(scores_used, 1)

            def evacuate(t):
                v.wait_ge(pT_psum, t + 1)
                if t >= 2:
                    v.wait_ge(pv_ready, t - 1)
                nc.vector.tensor_copy(PT[:, t % 2, 1, :].bitcast(F32), ps[0:SKV, 5, :]).then_inc(pT_low, 1)

            def divide(t):
                hf, k = t // CHUNKS, t % CHUNKS
                v.wait_ge(pv_ready, t + 1)
                if t >= 2:
                    v.wait_ge(o_ready, t - 1)
                n = CB * CH
                o = ps[:, 6, 0:32 * n].rearrange("p (i k) -> p i k", k=32)
                s, d = osum[:, t % 2], oden[:, t % 2]
                nc.vector.reciprocal(d, o[:, :, VC - 1])
                link(nc.vector.tensor_reduce(s, o[:, :, 0:3 * HD].rearrange("p i (a e) -> p i e a", a=3), axis=AX.X, op=ALU.add))
                nc.vector.tensor_tensor(On[:, hf, :, n * k:n * (k + 1)].rearrange("p e i -> p i e"), s,
                                        d.unsqueeze(2).broadcast_to([P, n, HD]), ALU.mult).then_inc(o_ready, 1)

            def weight_factors():
                v.wait_ge(wall_ready, 1)
                link(nc.vector.tensor_scalar(wpow[:, :], wall[:, :], 2.0 ** -60, None, ALU.max))
                link(nc.vector.tensor_scalar(wpow[:, :].bitcast(I32), wpow[:, :].bitcast(I32), 0x7F800000, None,
                                             ALU.bitwise_and))
                nc.vector.tensor_scalar(winv[:, :], wpow[:, :], 1.0 / (WSCALE * XSCALE), None, ALU.mult)
                link(nc.vector.reciprocal(wfac[:, :], wpow[:, :]))
                nc.vector.tensor_scalar(wfac[:, :], wfac[:, :], WSCALE, None, ALU.mult).then_inc(wfac_ready, 1)

            def gate_scores(hf):
                v.wait_ge(gexp_ready, hf + 1)
                link(nc.vector.tensor_scalar(ge[:, :, :], ge[:, :, :], 1.0, None, ALU.add))
                link(nc.vector.reciprocal(gs[:, :, :], ge[:, :, :]))
                link(nc.vector.tensor_tensor(gsc[:, :, :], gs[:, :, :], gb[:, :].unsqueeze(1).broadcast_to([P, RL, NE]), ALU.add))
                hi = gsc[:, :, :].rearrange("p r (g k) -> p (r g) k", g=NG)
                lo = None
                n = NE // NG // 2
                k = 0
                while n >= 1:
                    a, b = hi[:, :, 0:n], hi[:, :, n:2 * n]
                    nh = th[:, 2 * (k % 2), 0:RL * NG * n].rearrange("p (q n) -> p q n", n=n)
                    nl = th[:, 2 * (k % 2) + 1, 0:RL * NG * n].rearrange("p (q n) -> p q n", n=n)
                    tl = th[:, 4, 0:RL * NG * n].rearrange("p (q n) -> p q n", n=n)
                    tm = th[:, 5, 0:RL * NG * n].rearrange("p (q n) -> p q n", n=n)
                    nc.vector.tensor_tensor(nh, a, b, ALU.max)
                    if lo is None:
                        link(nc.vector.tensor_tensor(nl, a, b, ALU.min))
                    else:
                        nc.vector.tensor_tensor(tl, a, b, ALU.min)
                        link(nc.vector.tensor_tensor(tm, lo[:, :, 0:n], lo[:, :, n:2 * n], ALU.max))
                        link(nc.vector.tensor_tensor(nl, tl, tm, ALU.max))
                    hi, lo = nh, nl
                    n //= 2
                    k += 1
                g3 = grp[:, :, :]
                link(nc.vector.tensor_tensor(g3, hi.rearrange("p (r g) n -> p r (g n)", r=RL),
                                             lo.rearrange("p (r g) n -> p r (g n)", r=RL), ALU.add))

            def gate_weights(hf):
                g3 = grp[:, :, :]
                other = g3.unsqueeze(2).broadcast_to([P, RL, NG, NG])
                own = g3.unsqueeze(3).broadcast_to([P, RL, NG, NG])
                nc.vector.tensor_tensor(cmp[:, 0], other, own, ALU.is_gt)
                link(nc.vector.tensor_tensor(cmp[:, 1], other, own, ALU.is_equal))
                low4 = lower.rearrange("p (i j) -> p i j", i=NG).unsqueeze(1).broadcast_to([P, RL, NG, NG])
                link(nc.vector.tensor_tensor(cmp[:, 1], cmp[:, 1], low4, ALU.mult))
                link(nc.vector.tensor_tensor(cmp[:, 2], cmp[:, 0], cmp[:, 1], ALU.add))
                link(nc.vector.tensor_reduce(gcnt[:, :, :], cmp[:, 2], axis=AX.X, op=ALU.add))
                link(nc.vector.tensor_scalar(gcnt[:, :, :], gcnt[:, :, :], 1.5, None, ALU.is_lt))
                link(nc.vector.tensor_tensor(msk[:, :, :].rearrange("p r (g k) -> p r g k", g=NG),
                                             gsc[:, :, :].rearrange("p r (g k) -> p r g k", g=NG),
                                             gcnt[:, :, :].unsqueeze(3).broadcast_to([P, RL, NG, NE // NG]), ALU.mult))
                for r in range(RL):
                    i = nc.vector.max(top8[:, r], msk[:, r])
                link(i)
                for r in range(RL):
                    i = nc.vector.match_replace(out=repl[:, r], in_to_replace=top8[:, r], in_values=msk[:, r], imm_value=-3.0e38)
                link(i)
                link(nc.vector.tensor_tensor(repl[:, :, :], repl[:, :, :], msk[:, :, :], ALU.not_equal))
                link(nc.vector.tensor_tensor(wgt[:, :, :], gs[:, :, :], repl[:, :, :], ALU.mult))
                link(nc.vector.tensor_reduce(wsum[:, :], wgt[:, :, :], axis=AX.X, op=ALU.add))
                link(nc.vector.tensor_scalar(wsum[:, :], wsum[:, :], 1e-20, None, ALU.add))
                link(nc.vector.reciprocal(wsum[:, :], wsum[:, :]))
                link(nc.vector.tensor_scalar(wsum[:, :], wsum[:, :], ROUTED_SCALING, None, ALU.mult))
                link(nc.vector.tensor_tensor(wgt[:, :, :], wgt[:, :, :], wsum[:, :].unsqueeze(2).broadcast_to([P, RL, NE]), ALU.mult))
                if hf:
                    v.wait_ge(w3T_psum, hf)
                link(nc.vector.tensor_copy(w3[:, :, 0], wgt[:, :, :]))
                link(nc.vector.tensor_tensor(wres[:, :, :], wgt[:, :, :], w3[:, :, 0], ALU.subtract))
                link(nc.vector.tensor_copy(w3[:, :, 1], wres[:, :, :]))
                nc.vector.tensor_tensor(w3[:, :, 2], wres[:, :, :], w3[:, :, 1], ALU.subtract).then_inc(w3_ready, 1)


            def post(hf, at):
                step = POST[hf]
                if at == step["norm"]:
                    v.wait_ge(proj_psum, hf + 1)
                    link(nc.vector.tensor_tensor(x1[:, hf].rearrange("p l d -> p (l d)"),
                                                 x_sb[:, hf].rearrange("p l d -> p (l d)"), ps[:, MISC, :], ALU.add))
                    row_stats([x1[:, hf, r] for r in range(RL)])
                    for r in range(RL):
                        i = normalise_row(xn2[:, hf, r], x1[:, hf, r], r)
                    i.then_inc(xn2_ready, 1)
                    v.wait_ge(xn2_ready, hf + 1)
                if at == step["low"]:
                    v.wait_ge(xn2T_ready, hf + 1)
                    nc.vector.scalar_tensor_tensor(out=xl[:, hf], in0=ps[:, MISC, :], scalar=XSCALE, in1=xh[:, hf],
                                                   op0=ALU.mult, op1=ALU.subtract).then_inc(xlow_ready, 1)
                if at == step["gate"]:
                    gate_scores(hf)
                if at == step["gate"] + 1:
                    gate_weights(hf)

            v.wait_ge(s_x, 64)
            row_stats([x_sb[:, hf, r] for hf in range(HALVES) for r in range(RL)])
            for hf in range(HALVES):
                for r in range(RL):
                    i = normalise_row(xn[:, RL * hf + r], x_sb[:, hf, r], RL * hf + r)
                i.then_inc(xn_ready, 1)
            keys_split()
            for hf in range(HALVES):
                v.wait_ge(q_psum, hf + 1)
                split3(QT[:, hf, 0], QT[:, hf, 1], QT[:, hf, 2], ps[:, 6 + hf, :], res[:, 0:TOK]).then_inc(q_split, 1)
                v.wait_ge(q_split, hf + 1)
            v.wait_ge(vT_psum, 1)
            for bank in range(2):
                values_split(bank)
            v.wait_ge(k_spread, 16 * PARTS)
            key_order(range(0, B, 2))
            v.wait_ge(k_ordered, 2)
            v.wait_ge(q_dram, 32)
            shift(0)
            shift(1)
            v.wait_ge(s_egu, 32)
            nc.vector.tensor_reduce(wmax[:, :], egu[:, :, :, :].rearrange("p k u m -> p k (u m)"), axis=AX.X, op=ALU.max,
                                    apply_absolute_value=True).then_inc(wmax_ready, 1)
            for t in range(NT):
                if t >= 2:
                    divide(t - 2)
                if t + 2 < NT:
                    shift(t + 2)
                evacuate(t)
                if t == 3:
                    weight_factors()
                post(0, t)
            divide(NT - 2)
            divide(NT - 1)
            post(0, NT)
            v.wait_ge(wfac_ready, 1)
            for hf in range(HALVES):
                for u in range(UNITS):
                    n = hf * UNITS + u
                    v.wait_ge(silu_ready, n + 1)
                    v.wait_ge(u_psum, n + 1)
                    if n >= 2:
                        v.wait_ge(down_done, n - 1)
                    up_dst = h1 if u < PAIRS else hw
                    i = nc.vector.scalar_tensor_tensor(out=up_dst[:, n % 2], in0=ps[:, 2 + n % 2, :], scalar=winv[:, 1:2],
                                                       in1=sg[:, n % 2], op0=ALU.mult, op1=ALU.mult)
                    if u < PAIRS:
                        link(i)
                        v.wait_ge(wb_psum, hf * PAIRS + u + 1)
                        i = nc.vector.tensor_tensor(hw[:, n % 2], h1[:, n % 2], ps[:, 4 + n % 2, :], ALU.mult)
                    i.then_inc(h_ready, 1)
                    if hf == 0:
                        post(1, u)
                v.wait_ge(y_psum, hf + 1)
                nc.vector.tensor_tensor(y[:, hf].rearrange("p l d -> p (l d)"),
                                        x1[:, hf].rearrange("p l d -> p (l d)"), ps[:, MISC, :], ALU.add).then_inc(y_ready, 1)

        @block.tensor
        def _(pe):
            mm = nc.tensor.matmul
            pe.wait_ge(s_ctx, 32)
            for hf in range(HALVES):
                i = mm(ps[:, 4 + hf, 0:KV], wat[:, 2], ctx_sb[:, hf], start=True, stop=True)
            i.then_inc(v_psum, 1)
            for hf in range(HALVES):
                i = mm(ps[:, 2 + hf, 0:KV], wat[:, 1], ctx_sb[:, hf], start=True, stop=True)
            i.then_inc(k_psum, 1)
            pe.wait_ge(s_cf, 16)
            for hf in range(HALVES):
                pe.wait_ge(xn_ready, hf + 1)
                for r in range(RL):
                    i = nc.tensor.transpose(ps[:, hf, P * r:P * (r + 1)], xn[:, RL * hf + r], identf)
                i.then_inc(xnT_psum, 1)
            for hf in range(HALVES):
                pe.wait_ge(xnT_ready, hf + 1)
                mm(ps[:, 6 + hf, :], wat[:, 0], xnT[:, hf], start=True, stop=True).then_inc(q_psum, 1)

            def values():
                pe.wait_ge(v_ordered, 1)
                for h in range(NH):
                    i = nc.tensor.transpose(ps[0:SKV, 4 + h // 8, 64 * (h % 8):64 * (h % 8) + 64],
                                            VR[:, SKV * h:SKV * (h + 1)], identf[0:B * HD, 0:B * HD])
                i.then_inc(vT_psum, 1)

            def scores(t):
                hf, k = t // CHUNKS, t % CHUNKS
                if t >= 2:
                    pe.wait_ge(scores_used, t - 1)
                if k == 0:
                    pe.wait_ge(q_spread[hf], 16)
                    pe.wait_ge(k_ordered, 2)
                for g in range(CB):
                    bank = 2 * (t % 2) + g
                    mm(ps[:, bank, 0:CH * SKV], identb, maskneg, start=True, stop=False)
                    for i in range(CH):
                        n = CH * (CB * k + g) + i
                        h = n % NH
                        last = mm(ps[:, bank, SKV * i:SKV * (i + 1)], QS[:, hf, :, n],
                                  KR[:, hf * (B // HALVES) + n // NH, SKV * h:SKV * (h + 1)], start=False, stop=(i == CH - 1))
                last.then_inc(scores_ready, 1)

            def turn(t):
                pe.wait_ge(low_ready, t + 1)
                if t >= 1:
                    pe.wait_ge(pT_high, t)
                    pe.wait_ge(pT_low, t)
                for part, src in ((0, Ph), (1, Pl)):
                    for q in range(CB * CH):
                        last = nc.tensor.transpose(ps[0:SKV, 4 + part, 64 * q:64 * (q + 1)].bitcast(F16),
                                                   src[:, t % BUF, q // CH, q % CH, :], ch[:, :])
                last.then_inc(pT_psum, 1)

            def weigh(t):
                hf, k = t // CHUNKS, t % CHUNKS
                pe.wait_ge(pT_high, t + 1)
                pe.wait_ge(pT_low, t + 1)
                if t >= 1:
                    pe.wait_ge(o_ready, t)
                for q in range(CB * CH):
                    for part in range(2):
                        last = mm(ps[:, 6, 32 * q:32 * q + VC], PT[:, t % 2, part, P * q:P * (q + 1)],
                                  VV[:, CB * CH * t + q, :], start=(part == 0), stop=(part == 1))
                last.then_inc(pv_ready, 1)

            def post(hf, at):
                step = POST[hf]
                if at == step["proj"]:
                    pe.wait_ge(c_spread[hf], 16)
                    for r in range(RL):
                        last = mm(ps[:, MISC, P * r:P * (r + 1)],
                                  CT[:, hf, 2 * r:2 * r + 2, :].rearrange("p r n -> p (r n)"), wat[:, 3],
                                  start=True, stop=True)
                    last.then_inc(proj_psum, 1)
                if at == step["turn"]:
                    pe.wait_ge(xn2_ready, hf + 1)
                    for r in range(RL):
                        last = nc.tensor.transpose(ps[:, MISC, P * r:P * (r + 1)], xn2[:, hf, r], identf)
                    last.then_inc(xn2T_psum, 1)
                if at == step["logits"]:
                    pe.wait_ge(s_gw, 48)
                    pe.wait_ge(xlow_ready, hf + 1)
                    for r in range(RL):
                        last = mm(ps[:, MISC, NE * r:NE * (r + 1)], xn2T[:, hf, P * r:P * (r + 1)], gw[:, :],
                                  start=True, stop=True)
                    last.then_inc(logits_psum, 1)
                if at == step.get("w3", NT):
                    pe.wait_ge(w3_ready, hf + 1)
                    for r in range(RL):
                        last = nc.tensor.transpose(ps[0:3 * NE, MISC, 64 * r:64 * (r + 1)].bitcast(BF16),
                                                   w3[:, r].rearrange("p a e -> p (a e)"), identb)
                    last.then_inc(w3T_psum, 1)

            values()
            pe.wait_ge(s_cb, 32)
            pe.wait_ge(v_split, 2)
            pe.wait_ge(q_split, 2)
            for t in range(2):
                scores(t)
            for t in range(NT):
                if t + 2 < NT:
                    scores(t + 2)
                turn(t)
                if t >= 1:
                    weigh(t - 1)
                post(0, t)
            weigh(NT - 1)
            post(0, NT)
            pe.wait_ge(s_ed, 16)
            pe.wait_ge(wlow_ready, 10)
            pe.wait_ge(w3T_ready, 1)
            pe.wait_ge(o_ready, NT)

            def up(n):
                hf, u = n // UNITS, n % UNITS
                if u == 0 and hf:
                    pe.wait_ge(w3T_ready, 2)
                for k, ready in ((0, g_psum), (1, u_psum)):
                    if n >= 2:
                        pe.wait_ge(h_ready if k else silu_ready, n - 1)
                    w, wlo = wh[:, k, P * u:P * (u + 1)], wl[:, k, P * u:P * (u + 1)]
                    o = ps[:, 2 * k + n % 2, :]
                    mm(o, w, xh[:, hf], start=True, stop=False)
                    mm(o, w, xl[:, hf], start=False, stop=False)
                    mm(o, wlo, xh[:, hf], start=False, stop=True).then_inc(ready, 1)
                if u < PAIRS:
                    mm(ps[:, 4 + n % 2, :], sel[:, u], W3T[:, hf], start=True, stop=True).then_inc(wb_psum, 1)

            def down(n):
                hf, u = n // UNITS, n % UNITS
                pe.wait_ge(h_ready, n + 1)
                if u == 0 and hf:
                    pe.wait_ge(yT_ready, hf)
                mm(ps[:, 6, :], eds[:, u], hw[:, n % 2], start=(u == 0), stop=(u == UNITS - 1)).then_inc(down_done, 1)
                if hf == 0:
                    post(1, u)
                if u == UNITS - 1:
                    pe.wait_ge(yT_ready, hf + 1)
                    if hf:
                        pe.wait_ge(y_ready, hf)
                    for r in range(RL):
                        last = nc.tensor.transpose(ps[:, MISC, P * r:P * (r + 1)], yT[:, P * r:P * (r + 1)], identf)
                    last.then_inc(y_psum, 1)

            up(0)
            for n in range(HALVES * UNITS):
                if n + 1 < HALVES * UNITS:
                    up(n + 1)
                down(n)


def kernel(x, ctx_1024, L0_xattn_wq, L0_xattn_wk, L0_xattn_wv, L0_xattn_wproj, L0_ffn_gate_w, L0_ffn_gate_bias,
           L0_ffn_expert_gate, L0_ffn_expert_up, L0_ffn_expert_down, L0_ffn_shared_gate, L0_ffn_shared_up,
           L0_ffn_shared_down):
    import numpy as np
    import ml_dtypes
    import concourse.bacc as bacc
    from concourse.bass_utils import run_bass_kernel_spmd

    def a(t):
        return np.ascontiguousarray(t)

    x = a(x)
    ctxT = a(np.asarray(ctx_1024).reshape(B * SKV, D).T).reshape(D, HALVES, KV)

    def lane_first(t):
        return t.reshape(D, C, HD).transpose(0, 2, 1).reshape(D, D)

    wattn = [lane_first(np.asarray(w).T) for w in (L0_xattn_wq, L0_xattn_wk, L0_xattn_wv)]
    wattn = a(np.stack(wattn + [lane_first(np.asarray(L0_xattn_wproj)).T], 1))
    gwT = a(np.asarray(L0_ffn_gate_w).T)

    def rows(e, s):
        t = np.concatenate([np.asarray(e).reshape(-1, D), np.asarray(s)], 0)
        return a(t.T.reshape(D, UNITS, P))

    eg = rows(L0_ffn_expert_gate, L0_ffn_shared_gate)
    eu = rows(L0_ffn_expert_up, L0_ffn_shared_up)
    dn = np.concatenate([np.asarray(L0_ffn_expert_down).transpose(0, 2, 1).reshape(-1, D),
                         np.asarray(L0_ffn_shared_down).T], 0)
    ed = a(dn.reshape(UNITS, P, D).transpose(1, 0, 2))

    p = np.arange(P)
    r = p % RR
    query = C * (RL * (r % 2) + r // 2) + p // RR
    neg = np.where(np.arange(SKV)[None, :] > query[:, None], -1e30, 0.0)
    cbf16 = np.concatenate([np.eye(P)] + [neg] * CH, 1).astype(ml_dtypes.bfloat16)
    low = np.tril(np.ones((NG, NG)), -1).reshape(1, -1).repeat(P, 0)
    cf32 = np.concatenate([np.eye(P), low], 1).astype(np.float32)
    cf16 = np.eye(P).astype(np.float16)
    expert = 2 * np.arange(PAIRS)[:, None] + np.arange(P)[None, :] // 64
    csel = np.tile(np.arange(NE)[:, None, None] == expert[None], (3, 1, 1)).astype(ml_dtypes.bfloat16)

    arrays = {"x": x, "ctxT": ctxT, "wattn": wattn, "gwT": gwT, "gbias": a(L0_ffn_gate_bias), "eg": eg, "eu": eu,
              "ed": ed, "cf32": cf32, "cbf16": cbf16, "cf16": cf16, "csel": csel}
    nc = bacc.Bacc("TRN2", target_bir_lowering=False, num_devices=1)
    aps = [nc.dram_tensor(k, t.shape, mybir.dt.from_np(t.dtype), kind="ExternalInput").ap() for k, t in arrays.items()]
    out = nc.dram_tensor("out", (B, S, D), F32, kind="ExternalOutput").ap()
    block_kernel(nc, *aps, out)
    r = run_bass_kernel_spmd(nc, [arrays], core_ids=[0])
    return r.results[0]["out"]
```

```python
from contextlib import ExitStack

import concourse.bass as bass
from concourse import mybir

ALU = mybir.AluOpType
ACT = mybir.ActivationFunctionType
AX = mybir.AxisListType
F32 = mybir.dt.float32
I32 = mybir.dt.int32
BF16 = mybir.dt.bfloat16
F16 = mybir.dt.float16

P = 128
D = 128
B, S, SKV = 8, 128, 77
NH, HD = 16, 8
HALVES = 2
BH = B // HALVES * NH
TOK = B // HALVES * S
KV = B // HALVES * SKV
RR = S // NH
RL = TOK // P
C = D // HD
NKEY = SKV * C
CH = 4
CB = 2
CHUNKS = BH // (CH * CB)
NT = HALVES * CHUNKS
BUF = 4
NE = 32
NG = 4
PAIRS = NE // 2
UNITS = PAIRS + 1
ROUTED_SCALING = 2.5
EPS = 1e-5
XSCALE = 4096.0
WSCALE = 16384.0
SCALE = float(HD) ** -0.5
LN4096 = 8.317766166719343
PARTS = 3
ROWS = PARTS * PARTS * HD
VC = 3 * HD + 1


def block_kernel(nc, x, ctxT, wattn, gwT, gbias, eg, eu, ed, cf32, cbf16, cf16, csel, out):
    kd = nc.dram_tensor("kd", (HALVES, PARTS, HD, C, KV), BF16).ap()
    vd = nc.dram_tensor("vd", (B, HD, C, SKV), F32).ap()
    qd = nc.dram_tensor("qd", (HALVES, PARTS, HD, C, TOK), BF16).ap()
    od = nc.dram_tensor("od", (HALVES, C, RR, HD, BH), F32).ap()

    with ExitStack() as ctx:
        def sb(name, shape, dt=F32):
            return ctx.enter_context(nc.sbuf_tensor(name, shape, dt))

        def sem(name):
            return ctx.enter_context(nc.semaphore(name))

        x_sb = sb("x_sb", [P, HALVES, RL, D])
        ctx_sb = sb("ctx_sb", [P, HALVES, KV])
        wat = sb("wat", [P, 4, D])
        gw = sb("gw", [P, NE])
        gb = sb("gb", [P, NE])
        egu = sb("egu", [P, 2, UNITS, P])
        eds = sb("eds", [P, UNITS, P])
        VS = eds[0:B * HD].rearrange("p u m -> p (u m)")[:, 0:NKEY].rearrange("p (c n) -> p c n", c=C)
        cf = sb("cf", [P, P + NG * NG])
        cb = sb("cb", [P, P + CH * SKV], BF16)
        ch = sb("ch", [P, P], F16)
        sel = sb("sel", [3 * NE, PAIRS, P], BF16)
        identf = cf[:, 0:P]
        lower = cf[:, P:P + NG * NG]
        identb = cb[:, 0:P]
        maskneg = cb[:, P:P + CH * SKV]

        wall = sb("wall", [P, 2])
        wpow = sb("wpow", [P, 2])
        wfac = sb("wfac", [P, 2])
        winv = sb("winv", [P, 2])
        wh = sb("wh", [P, 2, UNITS * P], F16)
        wl = sb("wl", [P, 2, UNITS * P], F16)
        wmax = sb("wmax", [P, 2])
        wabs = wl[:, :, :].rearrange("p k n -> p (k n)").bitcast(F32)

        wgu = egu[:, :, :, :].rearrange("p k u m -> p k (u m)")

        stats = sb("stats", [P, HALVES * RL, 6])
        mv = sb("mv", [P, HALVES * RL, 2])
        lnv = sb("lnv", [P, HALVES * RL])
        lni = sb("lni", [P, HALVES * RL], I32)
        lny = sb("lny", [P, HALVES * RL])
        lnt = sb("lnt", [P, HALVES * RL])
        xn = sb("xn", [P, HALVES * RL, D])
        xn2 = xn[:, :, :].rearrange("p (f r) d -> p f r d", f=HALVES)
        y = xn2
        xnT = sb("xnT", [P, HALVES, TOK])
        xn2T = xnT
        xh = sb("xh", [P, HALVES, TOK], F16)
        xl = sb("xl", [P, HALVES, TOK], F16)

        QT = sb("QT", [P, HALVES, PARTS, TOK], BF16)
        KT = sb("KT", [P, HALVES, PARTS, KV], BF16)
        VT = sb("VT", [P, HALVES * KV])
        res = sb("res", [P, HALVES * KV])
        Sm = sb("Sm", [P, BUF, CB, CH, SKV])
        x1 = sb("x1", [P, HALVES, RL, D])
        CT = sb("CT", [P, HALVES, RR, BH])
        vres = CT.rearrange("p f r n -> p f (r n)")
        qres = x1[:, 1].rearrange("p l d -> p (l d)")
        QS = sb("QS", [ROWS, HALVES, C * RR, BH], BF16)
        KS = sb("KS", [P, HALVES, C, KV], BF16)
        P32 = KS[:, 0].rearrange("p c n -> p (c n)").bitcast(F32)[:, 0:BUF * CB * CH * SKV]\
            .rearrange("p (b g i j) -> p b g i j", b=BUF, g=CB, i=CH)
        KR = sb("KR", [ROWS, B, NKEY], BF16)
        VR = sb("VR", [B * HD, NKEY])
        VV = sb("VV", [SKV, B * NH, VC], BF16)
        mx = sb("mx", [P, BUF, CB * CH])
        Ph = sb("Ph", [P, BUF, CB, CH, SKV], F16)
        Pl = sb("Pl", [P, BUF, CB, CH, SKV], F16)
        PT = sb("PT", [SKV, 2, 2, CB * CH * P], F16)
        osum = sb("osum", [P, 2, CB * CH, HD])
        oden = sb("oden", [P, 2, CB * CH])
        On = QT[:, :].rearrange("p f a n -> p (f a n)").bitcast(F32)[:, 0:HALVES * HD * BH]\
            .rearrange("p (f e n) -> p f e n", f=HALVES, e=HD)
        bias12 = sb("bias12", [P, 1])

        wres = sb("wres", [P, RL, NE])
        gs = sb("gs", [P, RL, NE])
        ge = wres
        gsc = sb("gsc", [P, RL, NE])
        th = sb("th", [P, 6, RL * NG * 4])
        grp = sb("grp", [P, RL, NG])
        cmp = sb("cmp", [P, 2, RL, NG, NG])
        gcnt = sb("gcnt", [P, RL, NG])
        msk = sb("msk", [P, RL, NE])
        top8 = sb("top8", [P, RL, 8])
        repl = sb("repl", [P, RL, NE])
        wgt = sb("wgt", [P, RL, NE])
        wsum = sb("wsum", [P, RL])
        w3 = sb("w3", [P, RL, 3, NE], BF16)
        W3T = Sm.rearrange("p b g i j -> p (b g i j)")[0:3 * NE, 0:TOK].bitcast(BF16)\
            .rearrange("p (f n) -> p f n", f=HALVES)

        flat = egu[:, :, :, :].rearrange("p k u m -> p (k u m)")
        sg, h1, hw = (flat[:, 2 * TOK * i:2 * TOK * (i + 1)].rearrange("p (b n) -> p b n", b=2) for i in range(3))

        ps = ctx.enter_context(nc.psum_tensor("ps", [P, 8, 512], F32))
        MISC = 7

        s_cf = sem("s_cf")
        s_x = [sem(f"s_x{i}") for i in range(HALVES)]
        s_ctx = sem("s_ctx")
        s_gw = sem("s_gw")
        s_eg = sem("s_eg")
        s_eu = sem("s_eu")
        k_high = sem("k_high")
        k_rest = sem("k_rest")
        k_middle = sem("k_middle")
        s_ed = sem("s_ed")
        s_cb = sem("s_cb")
        consts_set = sem("consts_set")
        k1_ordered = sem("k1_ordered")
        dve = sem("dve")
        wmax_ready = sem("wmax_ready")
        wall_ready = sem("wall_ready")
        wfac_ready = sem("wfac_ready")
        whigh_ready = sem("whigh_ready")
        wlow_ready = sem("wlow_ready")
        wscaled = sem("wscaled")
        wlast_ready = sem("wlast_ready")
        xn_ready = sem("xn_ready")
        xnT_psum = sem("xnT_psum")
        xnT_ready = sem("xnT_ready")
        k_psum = sem("k_psum")
        v_psum = sem("v_psum")
        q_psum = sem("q_psum")
        k_split = sem("k_split")
        v_copied = sem("v_copied")
        q_split = sem("q_split")
        k_dram = [sem(f"k_dram{i}") for i in range(HALVES)]
        v_dram = sem("v_dram")
        q_dram = sem("q_dram")
        o_dram = sem("o_dram")
        k_spread = [sem(f"k_spread{i}") for i in range(HALVES)]
        v_spread = sem("v_spread")
        q_spread = [sem(f"q_spread{i}") for i in range(HALVES)]
        c_spread = [sem(f"c_spread{i}") for i in range(HALVES)]
        k_ordered = sem("k_ordered")
        v_ordered = sem("v_ordered")
        vT_psum = sem("vT_psum")
        v_split = sem("v_split")
        v_rest = sem("v_rest")
        v_middle = sem("v_middle")
        scores_ready = sem("scores_ready")
        scores_used = sem("scores_used")
        exps_ready = sem("exps_ready")
        low_ready = sem("low_ready")
        pT_psum = sem("pT_psum")
        pT_high = sem("pT_high")
        pT_low = sem("pT_low")
        pv_ready = sem("pv_ready")
        o_ready = sem("o_ready")
        proj_psum = sem("proj_psum")
        xn2_ready = sem("xn2_ready")
        xn2T_psum = sem("xn2T_psum")
        xn2T_ready = sem("xn2T_ready")
        xlow_ready = sem("xlow_ready")
        logits_psum = sem("logits_psum")
        gscore_ready = sem("gscore_ready")
        w3_ready = sem("w3_ready")
        w3T_psum = sem("w3T_psum")
        w3T_ready = sem("w3T_ready")
        g_psum = sem("g_psum")
        u_psum = sem("u_psum")
        wb_psum = sem("wb_psum")
        silu_ready = sem("silu_ready")
        h_ready = sem("h_ready")
        down_done = sem("down_done")
        y_ready = sem("y_ready")
        s_out = sem("s_out")

        def token_view(t, hf):
            v = t.rearrange("(f n) s d -> f (n s) d", f=HALVES)[hf]
            return v.rearrange("(a h l) d -> h a (l d)", h=2, l=RL)

        WN, W_EARLY, W0 = 4, 2, 1
        WLN, WLV, WLOW0, WLOW1 = 8, 4, 3, 6
        LOW_ACT = 3
        KEYS_ACT = (4, 5)

        POST = {0: dict(proj=11, turn=12.75, logits=13),
                1: dict(proj=2, turn=7, logits=9, w3=15)}
        PER_OP, PER_OP_END, PER_OP1 = 5, 2, 3

        block = ctx.enter_context(nc.Block())

        @block.sync
        def _(sp):
            def load_rows(hf):
                sp.dma_start(x_sb[:, hf].rearrange("p l d -> p (l d)"), token_view(x, hf)).then_inc(s_x[hf], 16)

            load_rows(0)
            sp.dma_start(ctx_sb[:, :, :], ctxT).then_inc(s_ctx, 16)
            sp.dma_start(wat[:, :, :], wattn).then_inc(s_ctx, 16)
            sp.dma_start(cf[:, :], cf32).then_inc(s_cf, 16)
            load_rows(1)
            sp.dma_start(egu[:, 0], eg).then_inc(s_eg, 16)
            sp.dma_start(egu[:, 1], eu).then_inc(s_eu, 16)
            sp.dma_start(cb[:, :], cbf16).then_inc(s_cb, 16)
            sp.dma_start(ch[:, :], cf16).then_inc(s_cb, 16)
            sp.wait_ge(k_split, 1)
            for hf in range(HALVES):
                sp.dma_start(kd[hf].rearrange("a e c n -> (e c) a n"), KT[:, hf]).then_inc(k_dram[hf], 16)
            sp.wait_ge(v_copied, 1)
            sp.dma_start(vd.rearrange("b e c n -> (e c) b n"), VT[:, :]).then_inc(v_dram, 16)
            def spread_keys(hf):
                sp.wait_ge(k_dram[hf], 16)
                for i in range(PARTS):
                    sp.dma_start(KS[PARTS * HD * i:PARTS * HD * (i + 1), hf].rearrange("p c n -> p (c n)"),
                                 kd[hf].rearrange("a e c n -> e a (c n)")).then_inc(k_spread[hf], 16)

            def store_queries(hf):
                sp.wait_ge(q_split, hf + 1)
                sp.dma_start(qd[hf].rearrange("a e c n -> (e c) a n"), QT[:, hf]).then_inc(q_dram, 16)

            def spread_queries(hf):
                sp.wait_ge(q_dram, 16 * (hf + 1))
                sp.dma_start(QS[:, hf].rearrange("p c n -> p (c n)"),
                             qd[hf].rearrange("a e c n -> (a e) (c n)").unsqueeze(1)
                             .broadcast_to([PARTS * HD, PARTS, C * TOK])).then_inc(q_spread[hf], 16)

            spread_keys(0)
            store_queries(0)
            sp.wait_ge(v_dram, 16)
            sp.dma_start(VS, vd.rearrange("b e c n -> (b e) c n")).then_inc(v_spread, 16)
            spread_keys(1)
            spread_queries(0)
            store_queries(1)
            spread_queries(1)
            sp.dma_start(gw[:, :], gwT).then_inc(s_gw, 16)
            sp.dma_start(gb[:, :], gbias.partition_broadcast(P)).then_inc(s_gw, 16)
            sp.dma_start(sel[:, :, :], csel).then_inc(s_gw, 16)
            sp.wait_ge(v_ordered, 1)
            sp.dma_start(eds[:, :, :], ed).then_inc(s_ed, 16)
            for hf in range(HALVES):
                sp.wait_ge(o_ready, CHUNKS * (hf + 1))
                sp.dma_start(od[hf].rearrange("c r e n -> (c r) e n"), On[:, hf]).then_inc(o_dram, 16)
                sp.wait_ge(o_dram, 16 * (hf + 1))
                sp.dma_start(CT[:, hf], od[hf].rearrange("c r e n -> e c r n")).then_inc(c_spread[hf], 16)
            for hf in range(HALVES):
                sp.wait_ge(y_ready, hf + 1)
                sp.dma_start(token_view(out, hf), y[:, hf].rearrange("p l d -> p (l d)")).then_inc(s_out, 16)
            sp.wait_ge(s_out, 16 * HALVES)

        def value_part(bank, k):
            return VV[:, :].rearrange("p (b h) k -> p h b k", h=NH)[:, NH // 2 * bank:NH // 2 * (bank + 1), :, HD * k:HD * (k + 1)]

        def value_rest(bank):
            return vres[0:SKV, bank].rearrange("p (h b e) -> p h b e", h=NH // 2, b=B)

        def evacuate_low(t, engine, copy):
            engine.wait_ge(pT_psum, t + 1)
            if t >= 2:
                engine.wait_ge(pv_ready, t - 1)
            copy(PT[:, t % 2, 1, :].bitcast(F32), ps[0:SKV, 5, :]).then_inc(pT_low, 1)

        @block.gpsimd
        def _(pool):
            nc.gpsimd.memset(bias12[:, :], LN4096).then_inc(consts_set, 1)
            pool.wait_ge(consts_set, 1)
            nc.gpsimd.memset(VV[:, :, VC - 1:VC], 1.0).then_inc(consts_set, 1)
            pool.wait_ge(wmax_ready, 2)
            nc.gpsimd.partition_all_reduce(wall[:, :], wmax[:, :], P, bass.bass_isa.ReduceOp.max).then_inc(wall_ready, 1)
            pool.wait_ge(wall_ready, 1)
            for bank in range(2):
                pool.wait_ge(v_rest, bank + 1)
                nc.gpsimd.tensor_copy(value_part(bank, 1), value_rest(bank)).then_inc(v_middle, 1)
                pool.wait_ge(v_middle, bank + 1)
                nc.gpsimd.tensor_tensor(value_part(bank, 2), value_rest(bank), value_part(bank, 1), ALU.subtract)\
                    .then_inc(v_split, 1)
                pool.wait_ge(v_split, bank + 1)
            pool.wait_ge(k_spread[1], 16 * PARTS)
            for t in range(NT):
                pool.wait_ge(exps_ready, t + 1)
                if t:
                    pool.wait_ge(low_ready, t)
                if t >= BUF:
                    pool.wait_ge(pT_psum, t - BUF + 1)
                nc.gpsimd.tensor_tensor(Pl[:, t % BUF], P32[:, t % BUF], Ph[:, t % BUF], ALU.subtract)\
                    .then_inc(low_ready, 1)
                if t < 6:
                    b, a = 4 + t // 3, 26 * (t % 3)
                    e = min(a + 26, SKV)
                    pool.wait_ge(low_ready, t + 1)
                    nc.gpsimd.tensor_copy(KR[:, b, C * a:C * e].rearrange("p (r c) -> p r c", c=C),
                                          KS[0:ROWS, 1, :, SKV * (b - 4) + a:SKV * (b - 4) + e].rearrange("p c r -> p r c"))\
                        .then_inc(k1_ordered, 1)
                    pool.wait_ge(k1_ordered, t + 1)
                f = WLV + (t - WLOW1) // 2
                if t >= WLOW1 and f < WLN:
                    a, b = f * UNITS * P // WLN, (f + 1) * UNITS * P // WLN
                    pool.wait_ge(low_ready, t + 1)
                    if (t - WLOW1) % 2 == 0:
                        pool.wait_ge(whigh_ready, 1 + f * WN // WLN)
                        nc.gpsimd.tensor_tensor(wgu[:, :, a:b], wgu[:, :, a:b],
                                                wfac[:, :].unsqueeze(2).broadcast_to([P, 2, b - a]), ALU.mult)\
                            .then_inc(wscaled, 1)
                        pool.wait_ge(wscaled, f - WLV + 1)
                    else:
                        nc.gpsimd.tensor_tensor(wl[:, :, a:b], wgu[:, :, a:b], wh[:, :, a:b], ALU.subtract)\
                            .then_inc(wlast_ready, 1)
                        pool.wait_ge(wlast_ready, f - WLV + 1)

        @block.scalar
        def _(act):
            def key_order(batches):
                for b in batches:
                    n = SKV * (b % 4)
                    i = nc.scalar.copy(KR[:, b].rearrange("p (r c) -> p r c", c=C),
                                       KS[0:ROWS, b // 4, :, n:n + SKV].rearrange("p c r -> p r c"))
                i.then_inc(k_ordered, 1)

            def exps(t):
                act.wait_ge(scores_used, t + 1)
                if t >= BUF:
                    act.wait_ge(pT_psum, t - BUF + 1)
                    act.wait_ge(low_ready, t - BUF + 1)
                b = t % BUF
                nc.scalar.activation(Ph[:, b], Sm[:, b], ACT.Exp, bias=bias12[:, 0:1], scale=SCALE)
                nc.scalar.activation(P32[:, b], Sm[:, b], ACT.Exp, bias=bias12[:, 0:1], scale=SCALE)\
                    .then_inc(exps_ready, 1)

            def weights_high(f):
                a, b = f * UNITS * P // WN, (f + 1) * UNITS * P // WN
                for k in range(2):
                    i = nc.scalar.activation(wh[:, k, a:b], wgu[:, k, a:b], ACT.Copy, scale=wfac[:, k:k + 1])
                i.then_inc(whigh_ready, 1)

            def post(hf, at):
                step = POST[hf]
                if at == step["turn"]:
                    act.wait_ge(xn2T_psum, hf + 1)
                    nc.scalar.copy(xn2T[:, hf], ps[:, MISC, :])
                    nc.scalar.mul(xh[:, hf], ps[:, MISC, :], XSCALE).then_inc(xn2T_ready, 1)
                if at == step["logits"]:
                    act.wait_ge(logits_psum, hf + 1)
                    if hf:
                        act.wait_ge(w3_ready, hf)
                    logits = ps[:, MISC, 0:RL * NE].rearrange("p (r e) -> p r e", e=NE)
                    if hf:
                        nc.scalar.activation(gs[:, :, :], logits, ACT.Sigmoid).then_inc(gscore_ready, 1)
                    else:
                        nc.scalar.activation(ge[:, :, :], logits, ACT.Exp, scale=-1.0).then_inc(gscore_ready, 1)
                if at == step.get("w3", NT):
                    act.wait_ge(w3T_psum, hf + 1)
                    nc.scalar.copy(W3T[:, hf], ps[0:3 * NE, MISC, 0:TOK // 2].bitcast(BF16)).then_inc(w3T_ready, 1)

            act.wait_ge(k_psum, 1)
            nc.scalar.copy(KT[:, :, 0], ps[:, 2:4, 0:KV]).then_inc(k_high, 1)
            act.wait_ge(k_rest, 1)
            nc.scalar.copy(KT[:, :, 1], res[:, :].rearrange("p (f n) -> p f n", f=HALVES)).then_inc(k_middle, 1)

            def magnitudes(k, loaded):
                act.wait_ge(loaded, 16)
                if k:
                    act.wait_ge(wmax_ready, 1)
                nc.scalar.activation(wabs, wgu[:, k], ACT.Abs, accum_out=wmax[:, k:k + 1]).then_inc(wmax_ready, 1)

            def rows_turned(hf):
                act.wait_ge(xnT_psum, hf + 1)
                nc.scalar.copy(xnT[:, hf], ps[:, 3 * hf, :]).then_inc(xnT_ready, 1)

            rows_turned(0)
            act.wait_ge(v_psum, 1)
            nc.scalar.copy(VT[:, :].rearrange("p (f n) -> p f n", f=HALVES), ps[:, 4:6, 0:KV]).then_inc(v_copied, 1)
            magnitudes(0, s_eg)
            magnitudes(1, s_eu)
            act.wait_ge(v_spread, 16)
            nc.scalar.copy(VR[:, :].rearrange("p (r c) -> p r c", c=C), VS.rearrange("p c r -> p r c")).then_inc(v_ordered, 1)
            rows_turned(1)
            act.wait_ge(k_spread[0], 16 * PARTS)
            key_order([2, 3])
            act.wait_ge(wfac_ready, 1)
            for f in range(W_EARLY):
                weights_high(f)
            act.wait_ge(consts_set, 1)
            exps(0)
            exps(1)
            for t in range(NT):
                if t + 2 < NT:
                    exps(t + 2)
                post(0, t - 0.5)
                post(0, t - 0.25)
                act.wait_ge(pT_psum, t + 1)
                if t >= 2:
                    act.wait_ge(pv_ready, t - 1)
                nc.scalar.copy(PT[:, t % 2, 0, :].bitcast(F32), ps[0:SKV, 4, :]).then_inc(pT_high, 1)
                if t >= LOW_ACT:
                    evacuate_low(t, act, nc.scalar.copy)
                if t in KEYS_ACT:
                    act.wait_ge(k_spread[1], 16 * PARTS)
                    key_order([6 + KEYS_ACT.index(t)])
                if 0 <= t - W0 < WN - W_EARLY:
                    weights_high(W_EARLY + t - W0)
                post(0, t)
            for hf in range(HALVES):
                for u in range(UNITS):
                    n = hf * UNITS + u
                    act.wait_ge(g_psum, n + 1)
                    if n >= 2:
                        act.wait_ge(h_ready, n - 1)
                    nc.scalar.activation(sg[:, n % 2], ps[:, n % 2, :], ACT.Silu, scale=winv[:, 0:1]).then_inc(silu_ready, 1)
                    if n == 1:
                        post(0, NT)
                    if hf == 0 and u:
                        post(1, u - 1)

        @block.vector
        def _(v):
            steps = [0]

            def link(ins):
                steps[0] += 1
                ins.then_inc(dve, 1)
                v.wait_ge(dve, steps[0])

            def after(ins):
                steps[0] += 1
                n = steps[0]
                ins.then_inc(dve, 1)
                yield
                v.wait_ge(dve, n)

            def row_stats(tiles):
                n = len(tiles)
                for r in range(n):
                    i = nc.vector.bn_stats(stats[:, r], tiles[r])
                    if r % 2:
                        yield from after(i)
                for r in range(n):
                    i = nc.vector.bn_aggr(mv[:, r], stats[:, r])
                yield from after(i)
                var, guess, y, t = lnv[:, 0:n], lni[:, 0:n], lny[:, 0:n], lnt[:, 0:n]
                yield from after(nc.vector.tensor_scalar(var, mv[:, 0:n, 1], EPS, None, ALU.add))
                yield from after(nc.vector.tensor_scalar(guess, var.bitcast(I32), 1, None, ALU.logical_shift_right))
                yield from after(nc.vector.tensor_scalar(y.bitcast(I32), guess, -1.0, 1597463007.0, ALU.mult, ALU.add))
                for _ in range(3):
                    yield from after(nc.vector.tensor_tensor(t, y, y, ALU.mult))
                    yield from after(nc.vector.scalar_tensor_tensor(out=t, in0=t, scalar=-0.5, in1=var, op0=ALU.mult, op1=ALU.mult))
                    yield from after(nc.vector.scalar_tensor_tensor(out=y, in0=t, scalar=1.5, in1=y, op0=ALU.add, op1=ALU.mult))

            def normalise_row(dst, src, r):
                return nc.vector.tensor_scalar(dst, src, mv[:, r, 0:1], lny[:, r:r + 1], ALU.subtract, ALU.mult)

            def split3(hi, mid, lo, src, tmp, done):
                yield from after(nc.vector.tensor_copy(hi, src))
                yield from after(nc.vector.tensor_tensor(tmp, src, hi, ALU.subtract))
                yield from after(nc.vector.tensor_copy(mid, tmp))
                nc.vector.tensor_tensor(lo, tmp, mid, ALU.subtract).then_inc(done, 1)
                yield

            def keys_split():
                rest = res[:, :].rearrange("p (f n) -> p f n", f=HALVES)
                v.wait_ge(k_high, 1)
                nc.vector.tensor_tensor(rest, ps[:, 2:4, 0:KV], KT[:, :, 0], ALU.subtract).then_inc(k_rest, 1)
                yield
                v.wait_ge(k_middle, 1)
                nc.vector.tensor_tensor(KT[:, :, 2], rest, KT[:, :, 1], ALU.subtract).then_inc(k_split, 1)
                yield

            def values_high(bank):
                v.wait_ge(vT_psum, 1)
                src = ps[0:SKV, 4 + bank, :].rearrange("p (h b e) -> p h b e", h=NH // 2, b=B)
                yield from after(nc.vector.tensor_copy(value_part(bank, 0), src))
                nc.vector.tensor_tensor(value_rest(bank), src, value_part(bank, 0), ALU.subtract).then_inc(v_rest, 1)
                yield

            def key_order(batches):
                for b in batches:
                    i = nc.vector.tensor_copy(KR[:, b].rearrange("p (r c) -> p r c", c=C),
                                              KS[0:ROWS, 0, :, SKV * b:SKV * (b + 1)].rearrange("p c r -> p r c"))
                i.then_inc(k_ordered, 1)

            def shift(t):
                v.wait_ge(scores_ready, t + 1)
                if t >= BUF:
                    v.wait_ge(exps_ready, t - BUF + 1)
                sc = ps[:, 2 * (t % 2):2 * (t % 2) + 2, 0:CH * SKV].rearrange("p g (i j) -> p g i j", j=SKV)
                m = mx[:, t % BUF].rearrange("p (g i) -> p g i", g=CB)
                yield from after(nc.vector.tensor_reduce(m, sc, axis=AX.X, op=ALU.max))
                nc.vector.tensor_tensor(Sm[:, t % BUF], sc, m.unsqueeze(3).broadcast_to([P, CB, CH, SKV]),
                                        ALU.subtract).then_inc(scores_used, 1)
                yield

            def divide(t):
                hf, k = t // CHUNKS, t % CHUNKS
                v.wait_ge(pv_ready, t + 1)
                if t >= 2:
                    v.wait_ge(o_ready, t - 1)
                n = CB * CH
                o = ps[:, 6, 0:32 * n].rearrange("p (i k) -> p i k", k=32)
                s, d = osum[:, t % 2], oden[:, t % 2]
                nc.vector.reciprocal(d, o[:, :, VC - 1])
                yield from after(nc.vector.tensor_reduce(s, o[:, :, 0:3 * HD].rearrange("p i (a e) -> p i e a", a=3),
                                                         axis=AX.X, op=ALU.add))
                nc.vector.tensor_tensor(On[:, hf, :, n * k:n * (k + 1)].rearrange("p e i -> p i e"), s,
                                        d.unsqueeze(2).broadcast_to([P, n, HD]), ALU.mult).then_inc(o_ready, 1)
                yield

            def weight_factors():
                v.wait_ge(wall_ready, 1)
                link(nc.vector.tensor_scalar(wpow[:, :], wall[:, :], 2.0 ** -60, None, ALU.max))
                link(nc.vector.tensor_scalar(wpow[:, :].bitcast(I32), wpow[:, :].bitcast(I32), 0x7F800000, None,
                                             ALU.bitwise_and))
                nc.vector.tensor_scalar(winv[:, :], wpow[:, :], 1.0 / (WSCALE * XSCALE), None, ALU.mult)
                link(nc.vector.reciprocal(wfac[:, :], wpow[:, :]))
                nc.vector.tensor_scalar(wfac[:, :], wfac[:, :], WSCALE, None, ALU.mult).then_inc(wfac_ready, 1)

            def weights_low(f):
                a, b = f * UNITS * P // WLN, (f + 1) * UNITS * P // WLN
                v.wait_ge(whigh_ready, 1 + f * WN // WLN)
                for k in range(2):
                    i = nc.vector.scalar_tensor_tensor(out=wl[:, k, a:b], in0=wgu[:, k, a:b], scalar=wfac[:, k:k + 1],
                                                       in1=wh[:, k, a:b], op0=ALU.mult, op1=ALU.subtract)
                i.then_inc(wlow_ready, 1)

            def gate_scores(hf):
                v.wait_ge(gscore_ready, hf + 1)
                if hf == 0:
                    yield from after(nc.vector.tensor_scalar(ge[:, :, :], ge[:, :, :], 1.0, None, ALU.add))
                    yield from after(nc.vector.reciprocal(gs[:, :, :], ge[:, :, :]))
                yield from after(nc.vector.tensor_tensor(gsc[:, :, :], gs[:, :, :], gb[:, :].unsqueeze(1).broadcast_to([P, RL, NE]), ALU.add))
                hi = gsc[:, :, :].rearrange("p r (g k) -> p (r g) k", g=NG)
                lo = None
                n = NE // NG // 2
                k = 0
                while n >= 1:
                    a, b = hi[:, :, 0:n], hi[:, :, n:2 * n]
                    nh = th[:, 2 * (k % 2), 0:RL * NG * n].rearrange("p (q n) -> p q n", n=n)
                    nl = th[:, 2 * (k % 2) + 1, 0:RL * NG * n].rearrange("p (q n) -> p q n", n=n)
                    tl = th[:, 4, 0:RL * NG * n].rearrange("p (q n) -> p q n", n=n)
                    tm = th[:, 5, 0:RL * NG * n].rearrange("p (q n) -> p q n", n=n)
                    nc.vector.tensor_tensor(nh, a, b, ALU.max)
                    if lo is None:
                        yield from after(nc.vector.tensor_tensor(nl, a, b, ALU.min))
                    else:
                        nc.vector.tensor_tensor(tl, a, b, ALU.min)
                        yield from after(nc.vector.tensor_tensor(tm, lo[:, :, 0:n], lo[:, :, n:2 * n], ALU.max))
                        yield from after(nc.vector.tensor_tensor(nl, tl, tm, ALU.max))
                    hi, lo = nh, nl
                    n //= 2
                    k += 1
                g3 = grp[:, :, :]
                yield from after(nc.vector.tensor_tensor(g3, hi.rearrange("p (r g) n -> p r (g n)", r=RL),
                                             lo.rearrange("p (r g) n -> p r (g n)", r=RL), ALU.add))

            def gate_weights(hf):
                g3 = grp[:, :, :]
                other = g3.unsqueeze(2).broadcast_to([P, RL, NG, NG])
                own = g3.unsqueeze(3).broadcast_to([P, RL, NG, NG])
                nc.vector.tensor_tensor(cmp[:, 0], other, own, ALU.is_gt)
                yield from after(nc.vector.tensor_tensor(cmp[:, 1], other, own, ALU.is_equal))
                low4 = lower.rearrange("p (i j) -> p i j", i=NG).unsqueeze(1).broadcast_to([P, RL, NG, NG])
                yield from after(nc.vector.tensor_tensor(cmp[:, 1], cmp[:, 1], low4, ALU.mult))
                yield from after(nc.vector.tensor_reduce(gcnt[:, :, :].rearrange("p r g -> p (r g)"),
                                                         cmp[:, :].rearrange("p k r i j -> p (r i) k j"),
                                                         axis=AX.XY, op=ALU.add))
                yield from after(nc.vector.scalar_tensor_tensor(
                    out=msk[:, :, :].rearrange("p r (g k) -> p (r g) k", g=NG),
                    in0=gcnt[:, :, :].rearrange("p r g -> p (r g)").unsqueeze(2).broadcast_to([P, RL * NG, NE // NG]),
                    scalar=1.5, in1=gsc[:, :, :].rearrange("p r (g k) -> p (r g) k", g=NG), op0=ALU.is_lt, op1=ALU.mult))
                for r in range(RL):
                    i = nc.vector.max(top8[:, r], msk[:, r])
                yield from after(i)
                for r in range(RL):
                    i = nc.vector.match_replace(out=repl[:, r], in_to_replace=top8[:, r], in_values=msk[:, r], imm_value=-3.0e38)
                yield from after(i)
                yield from after(nc.vector.tensor_tensor(repl[:, :, :], repl[:, :, :], msk[:, :, :], ALU.not_equal))
                yield from after(nc.vector.tensor_tensor(wgt[:, :, :], gs[:, :, :], repl[:, :, :], ALU.mult))
                yield from after(nc.vector.tensor_reduce(wsum[:, :], wgt[:, :, :], axis=AX.X, op=ALU.add))
                yield from after(nc.vector.tensor_scalar(wsum[:, :], wsum[:, :], 1e-20, 1.0 / ROUTED_SCALING, ALU.add, ALU.mult))
                yield from after(nc.vector.reciprocal(wsum[:, :], wsum[:, :]))
                if hf:
                    v.wait_ge(w3T_psum, hf)
                factor = wsum[:, :].unsqueeze(2).broadcast_to([P, RL, NE])
                nc.vector.tensor_tensor(w3[:, :, 0], wgt[:, :, :], factor, ALU.mult)
                yield from after(nc.vector.tensor_tensor(wgt[:, :, :], wgt[:, :, :], factor, ALU.mult))
                yield from after(nc.vector.tensor_tensor(wres[:, :, :], wgt[:, :, :], w3[:, :, 0], ALU.subtract))
                yield from after(nc.vector.tensor_copy(w3[:, :, 1], wres[:, :, :]))
                nc.vector.tensor_tensor(w3[:, :, 2], wres[:, :, :], w3[:, :, 1], ALU.subtract).then_inc(w3_ready, 1)


            now = [0]

            def from_step(hf, name):
                while now[0] < POST[hf][name] + hf:
                    yield

            def post(hf):
                yield from from_step(hf, "proj")
                v.wait_ge(proj_psum, hf + 1)
                yield from after(nc.vector.tensor_tensor(x1[:, hf].rearrange("p l d -> p (l d)"),
                                                         x_sb[:, hf].rearrange("p l d -> p (l d)"), ps[:, MISC, :], ALU.add))
                yield from row_stats([x1[:, hf, r] for r in range(RL)])
                for r in range(RL):
                    i = normalise_row(xn2[:, hf, r], x1[:, hf, r], r)
                    if r < RL - 1:
                        yield
                i.then_inc(xn2_ready, 1)
                yield
                v.wait_ge(xn2_ready, hf + 1)
                yield from from_step(hf, "turn")
                v.wait_ge(xn2T_ready, hf + 1)
                nc.vector.scalar_tensor_tensor(out=xl[:, hf], in0=ps[:, MISC, :], scalar=XSCALE, in1=xh[:, hf],
                                               op0=ALU.mult, op1=ALU.subtract).then_inc(xlow_ready, 1)
                yield
                yield from from_step(hf, "logits")
                yield from gate_scores(hf)
                yield from gate_weights(hf)

            def all_of(stage):
                for _ in stage:
                    pass

            def some_of(stage, n):
                for _ in range(n):
                    next(stage, None)

            def beside(stage, other, n=1):
                for _ in stage:
                    some_of(other, n)

            def together(*stages):
                while stages:
                    stages = [s for s in stages if next(s, NT) != NT]

            def rows_norm(hf):
                v.wait_ge(s_x[hf], 16)
                if hf:
                    v.wait_ge(xn_ready, hf)
                yield from row_stats([x_sb[:, hf, r] for r in range(RL)])
                for r in range(RL):
                    i = normalise_row(xn[:, RL * hf + r], x_sb[:, hf, r], r)
                i.then_inc(xn_ready, 1)
                yield

            def queries_split(hf):
                v.wait_ge(q_psum, hf + 1)
                yield from split3(QT[:, hf, 0], QT[:, hf, 1], QT[:, hf, 2], ps[:, 6 + hf, :], qres[:, :], q_split)

            all_of(rows_norm(0))
            norm = rows_norm(1)
            beside(keys_split(), norm)
            beside(queries_split(0), norm)
            all_of(norm)
            weight_factors()
            v.wait_ge(k_spread[0], 16 * PARTS)
            key_order([0, 1])
            together(values_high(0), values_high(1))
            all_of(shift(0))
            all_of(shift(1))
            all_of(queries_split(1))
            all_of(shift(2))
            stage = post(0)
            for t in range(NT):
                n = 0 if t <= POST[0]["proj"] else PER_OP if t < POST[0]["logits"] + 1 else PER_OP_END
                if t >= 2:
                    if t == 2:
                        v.wait_ge(q_dram, 32)
                    beside(divide(t - 2), stage, n)
                if t + 3 < NT:
                    beside(shift(t + 3), stage, n)
                now[0] = t - 0.25
                if t < LOW_ACT:
                    evacuate_low(t, v, nc.vector.tensor_copy)
                if 0 <= t - WLOW0 < WLV:
                    weights_low(t - WLOW0)
                now[0] = t
                some_of(stage, n)
            beside(divide(NT - 2), stage, PER_OP_END)
            beside(divide(NT - 1), stage, PER_OP_END)
            now[0] = NT
            for hf in range(HALVES):
                for u in range(UNITS):
                    m = hf * UNITS + u
                    n = PER_OP1 if hf == 0 and u > POST[1]["proj"] else 0
                    if m == 1:
                        all_of(stage)
                        stage, now[0] = post(1), 0
                    v.wait_ge(silu_ready, m + 1)
                    v.wait_ge(u_psum, m + 1)
                    if m >= 2:
                        v.wait_ge(down_done, m - 1)
                    up_dst = h1 if u else hw
                    i = nc.vector.scalar_tensor_tensor(out=up_dst[:, m % 2], in0=ps[:, 2 + m % 2, :], scalar=winv[:, 1:2],
                                                       in1=sg[:, m % 2], op0=ALU.mult, op1=ALU.mult)
                    if u:
                        part = after(i)
                        next(part)
                        some_of(stage, min(n, 1))
                        next(part, None)
                        v.wait_ge(wb_psum, hf * PAIRS + u)
                        i = nc.vector.tensor_tensor(hw[:, m % 2], h1[:, m % 2], ps[:, 4 + m % 2, :], ALU.mult)
                    i.then_inc(h_ready, 1)
                    now[0] = u
                    some_of(stage, n)
                if hf == 0:
                    now[0] = NT
                    all_of(stage)
                v.wait_ge(down_done, UNITS * (hf + 1))
                nc.vector.tensor_tensor(y[:, hf].rearrange("p l d -> p (l d)"),
                                        x1[:, hf].rearrange("p l d -> p (l d)"), ps[:, 6, :], ALU.add).then_inc(y_ready, 1)

        @block.tensor
        def _(pe):
            mm = nc.tensor.matmul
            pe.wait_ge(s_ctx, 32)
            for hf in range(HALVES):
                i = mm(ps[:, 2 + hf, 0:KV], wat[:, 1], ctx_sb[:, hf], start=True, stop=True)
            i.then_inc(k_psum, 1)
            pe.wait_ge(s_cf, 16)
            def queries(hf):
                pe.wait_ge(xn_ready, hf + 1)
                if hf:
                    pe.wait_ge(k_split, 1)
                for r in range(RL):
                    i = nc.tensor.transpose(ps[:, 3 * hf, P * r:P * (r + 1)], xn[:, RL * hf + r], identf)
                i.then_inc(xnT_psum, 1)
                if hf == 0:
                    for f in range(HALVES):
                        i = mm(ps[:, 4 + f, 0:KV], wat[:, 2], ctx_sb[:, f], start=True, stop=True)
                    i.then_inc(v_psum, 1)
                pe.wait_ge(xnT_ready, hf + 1)
                mm(ps[:, 6 + hf, :], wat[:, 0], xnT[:, hf], start=True, stop=True).then_inc(q_psum, 1)

            def values():
                pe.wait_ge(v_ordered, 1)
                for h in range(NH):
                    i = nc.tensor.transpose(ps[0:SKV, 4 + h // 8, 64 * (h % 8):64 * (h % 8) + 64],
                                            VR[:, SKV * h:SKV * (h + 1)], identf[0:B * HD, 0:B * HD])
                i.then_inc(vT_psum, 1)

            def scores(t):
                hf, k = t // CHUNKS, t % CHUNKS
                if t >= 2:
                    pe.wait_ge(scores_used, t - 1)
                if k == 0:
                    pe.wait_ge(q_spread[hf], 16)
                    pe.wait_ge(k_ordered, 2)
                if hf and k in (0, 2):
                    pe.wait_ge(k1_ordered, 3 if k == 0 else 6)
                if hf and k in (4, 6):
                    pe.wait_ge(k_ordered, 3 if k == 4 else 4)
                for g in range(CB):
                    bank = 2 * (t % 2) + g
                    mm(ps[:, bank, 0:CH * SKV], identb, maskneg, start=True, stop=False)
                    for i in range(CH):
                        n = CH * (CB * k + g) + i
                        h = n % NH
                        last = mm(ps[:, bank, SKV * i:SKV * (i + 1)], QS[:, hf, :, n],
                                  KR[:, hf * (B // HALVES) + n // NH, SKV * h:SKV * (h + 1)], start=False, stop=(i == CH - 1))
                last.then_inc(scores_ready, 1)

            def turn(t):
                pe.wait_ge(low_ready, t + 1)
                if t == 0:
                    pe.wait_ge(v_rest, 2)
                if t >= 1:
                    pe.wait_ge(pT_high, t)
                    pe.wait_ge(pT_low, t)
                for part, src in ((0, Ph), (1, Pl)):
                    for q in range(CB * CH):
                        last = nc.tensor.transpose(ps[0:SKV, 4 + part, 64 * q:64 * (q + 1)].bitcast(F16),
                                                   src[:, t % BUF, q // CH, q % CH, :], ch[:, :])
                last.then_inc(pT_psum, 1)

            def weigh(t):
                hf, k = t // CHUNKS, t % CHUNKS
                pe.wait_ge(pT_high, t + 1)
                pe.wait_ge(pT_low, t + 1)
                if t == 0:
                    pe.wait_ge(v_split, 2)
                if t >= 1:
                    pe.wait_ge(o_ready, t)
                else:
                    pe.wait_ge(q_split, 1)
                for q in range(CB * CH):
                    for part in range(2):
                        last = mm(ps[:, 6, 32 * q:32 * q + VC], PT[:, t % 2, part, P * q:P * (q + 1)],
                                  VV[:, CB * CH * t + q, :], start=(part == 0), stop=(part == 1))
                last.then_inc(pv_ready, 1)

            def post(hf, at):
                step = POST[hf]
                if at == step["proj"]:
                    pe.wait_ge(c_spread[hf], 16)
                    for r in range(RL):
                        last = mm(ps[:, MISC, P * r:P * (r + 1)],
                                  CT[:, hf, 2 * r:2 * r + 2, :].rearrange("p r n -> p (r n)"), wat[:, 3],
                                  start=True, stop=True)
                    last.then_inc(proj_psum, 1)
                if at == step["turn"]:
                    pe.wait_ge(xn2_ready, hf + 1)
                    for r in range(RL):
                        last = nc.tensor.transpose(ps[:, MISC, P * r:P * (r + 1)], xn2[:, hf, r], identf)
                    last.then_inc(xn2T_psum, 1)
                if at == step["logits"]:
                    pe.wait_ge(s_gw, 48)
                    pe.wait_ge(xlow_ready, hf + 1)
                    for r in range(RL):
                        last = mm(ps[:, MISC, NE * r:NE * (r + 1)], xn2T[:, hf, P * r:P * (r + 1)], gw[:, :],
                                  start=True, stop=True)
                    last.then_inc(logits_psum, 1)
                if at == step.get("w3", NT):
                    pe.wait_ge(w3_ready, hf + 1)
                    for r in range(RL):
                        last = nc.tensor.transpose(ps[0:3 * NE, MISC, 64 * r:64 * (r + 1)].bitcast(BF16),
                                                   w3[:, r].rearrange("p a e -> p (a e)"), identb)
                    last.then_inc(w3T_psum, 1)

            queries(0)
            values()
            queries(1)
            pe.wait_ge(s_cb, 32)
            for t in range(3):
                scores(t)
            for t in range(NT):
                if t + 3 < NT:
                    scores(t + 3)
                post(0, t - 0.5)
                turn(t)
                post(0, t - 0.25)
                if t >= 1:
                    weigh(t - 1)
                post(0, t)
            pe.wait_ge(wlow_ready, WLV)
            pe.wait_ge(wlast_ready, WLN - WLV)
            pe.wait_ge(scores_used, NT)

            def up(n):
                hf, u = n // UNITS, (n % UNITS - 1) % UNITS
                if u == PAIRS:
                    pe.wait_ge(xlow_ready, hf + 1)
                for k, ready in ((0, g_psum), (1, u_psum)):
                    if n >= 2:
                        pe.wait_ge(h_ready if k else silu_ready, n - 1)
                    w, wlo = wh[:, k, P * u:P * (u + 1)], wl[:, k, P * u:P * (u + 1)]
                    o = ps[:, 2 * k + n % 2, :]
                    mm(o, w, xh[:, hf], start=True, stop=False)
                    mm(o, w, xl[:, hf], start=False, stop=False)
                    mm(o, wlo, xh[:, hf], start=False, stop=True).then_inc(ready, 1)

            def routing(n):
                hf, u = n // UNITS, n % UNITS - 1
                if u == 0:
                    pe.wait_ge(w3T_ready, hf + 1)
                if n == 1:
                    pe.wait_ge(pT_high, NT)
                    pe.wait_ge(pT_low, NT)
                if u >= 0:
                    mm(ps[:, 4 + n % 2, :], sel[:, u], W3T[:, hf], start=True, stop=True).then_inc(wb_psum, 1)

            def down(n):
                hf, at = n // UNITS, n % UNITS
                u = (at - 1) % UNITS
                pe.wait_ge(h_ready, n + 1)
                if at == 0:
                    if hf:
                        pe.wait_ge(y_ready, hf)
                    else:
                        pe.wait_ge(o_ready, NT)
                for r in range(RL):
                    last = mm(ps[:, 6, P * r:P * (r + 1)], hw[:, n % 2, P * r:P * (r + 1)], eds[:, u],
                              start=(at == 0 and r == 0), stop=(at == UNITS - 1 and r == RL - 1))
                last.then_inc(down_done, 1)
                if hf == 0:
                    post(1, at)

            up(0)
            weigh(NT - 1)
            pe.wait_ge(s_ed, 16)
            for n in range(HALVES * UNITS):
                if n + 1 < HALVES * UNITS:
                    up(n + 1)
                    if n == 0:
                        post(0, NT)
                    routing(n + 1)
                down(n)


def kernel(x, ctx_1024, L0_xattn_wq, L0_xattn_wk, L0_xattn_wv, L0_xattn_wproj, L0_ffn_gate_w, L0_ffn_gate_bias,
           L0_ffn_expert_gate, L0_ffn_expert_up, L0_ffn_expert_down, L0_ffn_shared_gate, L0_ffn_shared_up,
           L0_ffn_shared_down):
    import numpy as np
    import ml_dtypes
    import concourse.bacc as bacc
    from concourse.bass_utils import run_bass_kernel_spmd

    def a(t):
        return np.ascontiguousarray(t)

    x = a(x)
    ctxT = a(np.asarray(ctx_1024).reshape(B * SKV, D).T).reshape(D, HALVES, KV)

    def lane_first(t):
        return t.reshape(D, C, HD).transpose(0, 2, 1).reshape(D, D)

    wattn = [lane_first(np.asarray(w).T) for w in (L0_xattn_wq, L0_xattn_wk, L0_xattn_wv)]
    wattn = a(np.stack(wattn + [lane_first(np.asarray(L0_xattn_wproj)).T], 1))
    gwT = a(np.asarray(L0_ffn_gate_w).T)

    def rows(e, s):
        t = np.concatenate([np.asarray(e).reshape(-1, D), np.asarray(s)], 0)
        return a(t.T.reshape(D, UNITS, P))

    eg = rows(L0_ffn_expert_gate, L0_ffn_shared_gate)
    eu = rows(L0_ffn_expert_up, L0_ffn_shared_up)
    dn = np.concatenate([np.asarray(L0_ffn_expert_down).transpose(0, 2, 1).reshape(-1, D),
                         np.asarray(L0_ffn_shared_down).T], 0)
    ed = a(dn.reshape(UNITS, P, D).transpose(1, 0, 2))

    p = np.arange(P)
    r = p % RR
    query = C * (RL * (r % 2) + r // 2) + p // RR
    neg = np.where(np.arange(SKV)[None, :] > query[:, None], -1e30, 0.0)
    cbf16 = np.concatenate([np.eye(P)] + [neg] * CH, 1).astype(ml_dtypes.bfloat16)
    low = np.tril(np.ones((NG, NG)), -1).reshape(1, -1).repeat(P, 0)
    cf32 = np.concatenate([np.eye(P), low], 1).astype(np.float32)
    cf16 = np.eye(P).astype(np.float16)
    expert = 2 * np.arange(PAIRS)[:, None] + np.arange(P)[None, :] // 64
    csel = np.tile(np.arange(NE)[:, None, None] == expert[None], (3, 1, 1)).astype(ml_dtypes.bfloat16)

    arrays = {"x": x, "ctxT": ctxT, "wattn": wattn, "gwT": gwT, "gbias": a(L0_ffn_gate_bias), "eg": eg, "eu": eu,
              "ed": ed, "cf32": cf32, "cbf16": cbf16, "cf16": cf16, "csel": csel}
    nc = bacc.Bacc("TRN2", target_bir_lowering=False, num_devices=1)
    aps = [nc.dram_tensor(k, t.shape, mybir.dt.from_np(t.dtype), kind="ExternalInput").ap() for k, t in arrays.items()]
    out = nc.dram_tensor("out", (B, S, D), F32, kind="ExternalOutput").ap()
    block_kernel(nc, *aps, out)
    r = run_bass_kernel_spmd(nc, [arrays], core_ids=[0])
    return r.results[0]["out"]
```
